# Optimizing a Trainium2 kernel written in Bass

```python
import numpy as np
import jax
import jax.numpy as jnp

def _softmax(x, axis=-1):
    return jax.nn.softmax(x, axis=axis)

def _gelu(x):
    return jax.nn.gelu(x, approximate=True)

def _silu(x):
    return jax.nn.silu(x)

def _sigmoid(x):
    return jax.nn.sigmoid(x)

def _layernorm(x, axis=-1, eps=1e-05):
    m = jnp.mean(x, axis=axis, keepdims=True)
    v = jnp.var(x, axis=axis, keepdims=True)
    return (x - m) / jnp.sqrt(v + eps)

def _scatter_add(tgt, idx, src, axis=0):
    return tgt.at[idx].add(src)

def _segment_sum(src, seg, n):
    return jax.ops.segment_sum(src, seg, n)
kernel_name = 'mk_adj_resnorm_d2_adj_r2_43e054'

def setup_inputs(seed: int=0):
    np.random.seed(seed)
    _w = jnp.asarray

    def _rec_inputs():
        import jax
        import jax.numpy as jnp
        _gk = jax.random.key(seed)
        x = -9.806e-05 + 1 * jax.random.normal(jax.random.fold_in(_gk, 1), (4096, 64), jnp.float32)
        _w = (1.0 + jnp.arange(4096, dtype=jnp.float32)) ** (-0.5)
        _w = _w / _w.mean()
        _pij = jnp.clip(0.00195312 * _w[:, None] * _w[None, :], 0.0, 1.0)
        _a = jax.random.uniform(jax.random.fold_in(_gk, 2), (4096, 4096)) < _pij
        adj = _a.astype(jnp.int32)
        return (x, adj)
    x, adj = _rec_inputs()

    def _L0_gnn_setup():
        import jax, jax.numpy as jnp
        import numpy as np
        ALPHA = 0.2
        NEG_BIG = -9000000000000000.0
        key = jax.random.key(seed)
        k1, k2, k3, k4, k5 = jax.random.split(key, 5)
        N, M, F_in, F_out = (4096, 4096, 64, 64)
        item_embs = jax.random.normal(k1, (N, F_in), dtype=jnp.float32)
        entity_embs = jax.random.normal(k2, (M, F_in), dtype=jnp.float32)
        adj = jax.random.randint(k3, (N, M), 0, 2, dtype=jnp.int32)
        W = jax.random.normal(k4, (F_in, F_out), dtype=jnp.float32)
        a = jax.random.normal(k5, (2 * F_out, 1), dtype=jnp.float32)
        return {'item_embs': item_embs, 'entity_embs': entity_embs, 'adj': adj, 'W': W, 'a': a}
    _L0_gnn_all = _L0_gnn_setup()
    _L0_gnn_in = {k: v for k, v in _L0_gnn_all.items() if k in ('entity_embs', 'W', 'a')}
    del _L0_gnn_all

    def _L1_gnn_setup():
        import jax, jax.numpy as jnp
        import numpy as np
        N = 4096
        F_IN = 64
        F_OUT = 64
        ALPHA = 0.2
        NEG_INF = -9000000000000000.0
        key = jax.random.key(seed)
        k1, k2, k3, k4 = jax.random.split(key, 4)
        h = jax.random.normal(k1, (N, F_IN), dtype=jnp.float32)
        adj = jax.random.randint(k2, (N, N), 0, 2, dtype=jnp.int32)
        W = jax.random.normal(k3, (F_OUT, F_IN), dtype=jnp.float32) * (1.0 / np.sqrt(F_IN))
        a = jax.random.normal(k4, (2 * F_OUT,), dtype=jnp.float32) * (1.0 / np.sqrt(2 * F_OUT))
        return {'h': h, 'adj': adj, 'W': W, 'a': a}
    _L1_gnn_all = _L1_gnn_setup()
    _L1_gnn_in = {k: v for k, v in _L1_gnn_all.items() if k in ('W', 'a')}
    del _L1_gnn_all
    return {'x': x, 'adj': adj, 'L0_gnn_entity_embs': _L0_gnn_in['entity_embs'], 'L0_gnn_W': _L0_gnn_in['W'], 'L0_gnn_a': _L0_gnn_in['a'], 'L1_gnn_W': _L1_gnn_in['W'], 'L1_gnn_a': _L1_gnn_in['a']}

def reference(x, adj, L0_gnn_entity_embs, L0_gnn_W, L0_gnn_a, L1_gnn_W, L1_gnn_a):
    import jax
    import jax.numpy as jnp

    def _L0_gnn_ref(item_embs, entity_embs, adj, W, a):
        import jax, jax.numpy as jnp
        import numpy as np
        ALPHA = 0.2
        NEG_BIG = -9000000000000000.0
        F_out = W.shape[1]
        Wh = item_embs @ W
        We = entity_embs @ W
        a1 = a[:F_out, 0]
        a2 = a[F_out:, 0]
        scores = (Wh @ a1)[:, None] + (We @ a2)[None, :]
        e = jnp.where(scores > 0, scores, ALPHA * scores)
        e = jnp.where(adj > 0, e, NEG_BIG)
        attention = jax.nn.softmax(e, axis=1)
        entity_emb_weighted = attention @ entity_embs
        h_prime = entity_emb_weighted + item_embs
        return jax.nn.elu(h_prime)

    def _L1_gnn_ref(h, adj, W, a):
        import jax, jax.numpy as jnp
        import numpy as np
        N = 4096
        F_IN = 64
        F_OUT = 64
        ALPHA = 0.2
        NEG_INF = -9000000000000000.0
        Wh = h @ W.T
        a1, a2 = (a[:F_OUT], a[F_OUT:])
        src = Wh @ a1
        dst = Wh @ a2
        e = jax.nn.leaky_relu(src[:, None] + dst[None, :], negative_slope=ALPHA)
        scores = jnp.where(adj > 0, e, NEG_INF)
        attention = jax.nn.softmax(scores, axis=1)
        h_prime = attention @ Wh
        return jax.nn.elu(h_prime)
    x = _layernorm(x + _L0_gnn_ref(x, L0_gnn_entity_embs, adj, L0_gnn_W, L0_gnn_a), axis=-1)
    x = _layernorm(x + _L1_gnn_ref(x, adj, L1_gnn_W, L1_gnn_a), axis=-1)
    return x

_drawn_inputs = setup_inputs


def setup_inputs(seed=0):
    import zlib

    import numpy as np

    out = dict(_drawn_inputs(seed))
    spreads = {}
    factors = {}
    for name, (base, spread) in spreads.items():
        noise = np.random.default_rng([zlib.crc32(name.encode()), seed]).standard_normal(out[name].shape)
        drawn = base * np.exp(spread * noise) if base else spread * noise
        out[name] = jnp.asarray(drawn.astype(out[name].dtype))
    for name, factor in factors.items():
        out[name] = (out[name] * factor).astype(out[name].dtype)
    return out
```

```python
from contextlib import ExitStack

import concourse.bass as bass
from concourse import mybir

ALU = mybir.AluOpType
ACT = mybir.ActivationFunctionType
AX = mybir.AxisListType
F32 = mybir.dt.float32
BF16 = mybir.dt.bfloat16
I32 = mybir.dt.int32
U8 = mybir.dt.uint8

P = 128
SLOPE = 0.2
EPS = 1e-5
SHRINK = 2.0 ** -40
BIG = 2.0 ** 60


def two_attention_layers(nc, x, adj, e, eT, xT, w0T, a0, w1, w1T, a1, out):
    N, F = x.shape
    T = N // P
    GT = 8
    G = T // GT
    GW = GT * P
    H = N // 2
    BANK = 512
    VW = F + 1
    SIX = 6
    LEAD = GT // 2 * SIX

    with ExitStack() as ctx:
        def sb(name, shape, dt):
            return ctx.enter_context(nc.sbuf_tensor(name, shape, dt))

        def sem(name):
            return ctx.enter_context(nc.semaphore(name))

        absent = sb("absent", [P, 2 * GT, N], BF16)
        edges = sb("edges", [P, 2, H], I32)
        d_row = sb("d_row", [P, N], F32)
        s_row = sb("s_row", [P, 2, GW], F32)
        probs = sb("probs", [P, 2, GW], F32)
        nodes = sb("nodes", [P, T, F], F32)
        values = sb("values", [P, T, VW], F32)
        values_now = sb("values_now", [P, 2, VW], F32)
        unused = sb("unused", [P, H], U8)
        u_rows = sb("u_rows", [P, GW], BF16)
        attended = sb("attended", [P, GT, VW], F32)
        tmp = sb("tmp", [P, 2, GT, F], F32)
        tmp_a, tmp_b = tmp[:, 0, :, :], tmp[:, 1, :, :]
        acc_sb = tmp[0:VW, :, :, :].rearrange("p a k f -> p (a k f)")
        ident = sb("ident", [P, P], F32)
        ident_b = sb("ident_b", [P, P], BF16)
        minus_big = sb("minus_big", [P, P], BF16)
        ones = sb("ones", [P, P], F32)
        pick = sb("pick", [P, 2, P], BF16)
        value_sum = sb("value_sum", [P, VW], F32)
        d_col = sb("d_col", [P, T], F32)
        nd8_col = sb("nd8_col", [P, T], F32)
        s_col = sb("s_col", [P, T], F32)
        s8_col = sb("s8_col", [P, T], F32)
        s2_col = sb("s2_col", [P, T], F32)
        low = sb("low", [P, 2, GT], F32)
        lowest = sb("lowest", [P, GT], F32)
        empty = sb("empty", [P, 2, GT], F32)
        mz = sb("mz", [P, 6, GT], F32)
        u_parts = sb("u_parts", [P, GT, 3], BF16)
        dens = sb("dens", [P, 2, GT], F32)
        stats = sb("stats", [P, 4, GT], F32)
        half_neg = sb("half_neg", [P, GT], F32)
        w0T_sb, w1_sb = tmp_b[0:F, 0, :], tmp_b[0:F, 1, :]
        a_sb = tmp_b[0:F, 2, 0:4].rearrange("f (l c) -> f l c", l=2)
        a_rep = tmp_a[0:F, 0:4, :].rearrange("f (l h) c -> f l (h c)", l=2)
        w_rep = sb("w_rep", [F, 2, P], F32)
        w_src = sb("w_src", [F, 2], F32)
        into1 = sb("into1", [F, F + 2], F32)
        turned = probs[0:F, :, 0:BANK]

        work = [ctx.enter_context(nc.psum_tensor(f"work{i}", [P, GW], F32)) for i in range(2)]
        acc = ctx.enter_context(nc.psum_tensor("acc", [P, 2, BANK], F32))
        misc = ctx.enter_context(nc.psum_tensor("misc", [P, 2, BANK], F32))
        eT_sb = absent[0:F, GT:GT + 2, :].rearrange("p a b -> p (a b)").bitcast(F32)
        xT_sb = absent[0:F, GT + 2:GT + 4, :].rearrange("p a b -> p (a b)").bitcast(F32)

        weights_in = sem("weights_in")
        nodes_in = sem("nodes_in")
        columns_in = sem("columns_in")
        chunk_in = [sem("chunk_in0"), sem("chunk_in1")]
        chunk_masked = sem("chunk_masked")
        consts_made = sem("consts_made")
        ones_made = sem("ones_made")
        reps_made = sem("reps_made")
        weights_done = sem("weights_done")
        weights_kept = sem("weights_kept")
        turned_done = sem("turned_done")
        turned_kept = sem("turned_kept")
        node_done = sem("node_done")
        node_kept = sem("node_kept")
        sum_done = sem("sum_done")
        sum_kept = sem("sum_kept")
        cols_made = sem("cols_made")
        row_low = sem("row_low")
        lowest_made = sem("lowest_made")
        pool_step = sem("pool_step")
        parts_made = sem("parts_made")
        diag_made = sem("diag_made")
        spread_done = sem("spread_done")
        spread_kept = sem("spread_kept")
        rows_done = sem("rows_done")
        rows_kept = sem("rows_kept")
        filled = sem("filled")
        scored = sem("scored")
        exped = sem("exped")
        used = sem("used")
        acc_kept = sem("acc_kept")
        acc_turned = sem("acc_turned")
        attended_made = sem("attended_made")
        den_made = sem("den_made")
        neg_made = sem("neg_made")
        neg_exped = sem("neg_exped")
        y_made = sem("y_made")
        mean_made = sem("mean_made")
        square_made = sem("square_made")
        var_made = sem("var_made")
        normed = sem("normed")
        stored = sem("stored")

        block = ctx.enter_context(nc.Block())

        def by_tile(a):
            return a.rearrange("(t p) f -> p t f", p=P)

        @block.sync
        def _(sp):
            for to, frm in ((w0T_sb, w0T), (w1_sb, w1), (into1[:, 0:F], w1T),
                            (a_sb[:, 0, :], a0), (a_sb[:, 1, :], a1)):
                sp.dma_start(to, frm).then_inc(weights_in, 16)
            sp.dma_start(eT_sb, eT).then_inc(columns_in, 16)
            sp.dma_start(xT_sb, xT).then_inc(columns_in, 16)

            def load_tile(layer, t, first):
                for half in range(2):
                    if not first:
                        sp.wait_ge(chunk_masked, 2 * T * layer + 2 * t + half - 1)
                    sp.dma_start(edges[:, half, :],
                                 adj[bass.ds(t * P, P), half * H:(half + 1) * H]
                                 ).then_inc(chunk_in[half], 16)

            load_tile(0, 0, True)
            sp.dma_start(nodes[:, :, :], by_tile(x)).then_inc(nodes_in, 16)
            sp.dma_start(values[:, :, 0:F], by_tile(e)).then_inc(nodes_in, 16)
            with sp.Fori(1, T) as t:
                load_tile(0, t, False)
            with sp.Fori(0, T) as t:
                load_tile(1, t, False)
            for g in range(G):
                sp.wait_ge(normed, G + g + 1)
                sp.dma_start(by_tile(out)[:, g * GT:(g + 1) * GT, :],
                             nodes[:, g * GT:(g + 1) * GT, :]).then_inc(stored, 16)
            sp.wait_ge(stored, 16 * G)

        @block.gpsimd
        def _(pool):
            steps = [0]

            def mine(ins):
                steps[0] += 1
                ins.then_inc(pool_step, 1)
                pool.wait_ge(pool_step, steps[0])

            mine(pool.memset(ident[:, :], 0.0))
            mine(pool.affine_select(out=ident[:, :], in_=ident[:, :], compare_op=ALU.not_equal,
                                    fill=1.0, base=0, pattern=[[-1, P]], channel_multiplier=1))
            mine(pool.tensor_copy(ident_b[:, :], ident[:, :]))
            mine(pool.tensor_scalar(minus_big[:, :], ident[:, :], -BIG, None, ALU.mult))
            pool.memset(half_neg[:, :], -0.5).then_inc(consts_made, 1)

            def columns(layer):
                pool.wait_ge(node_kept, 8 * (layer + 1))
                mine(pool.tensor_scalar(nd8_col[:, :], d_col[:, :], -(1 - SLOPE), None, ALU.mult))
                mine(pool.tensor_scalar(s8_col[:, :], s_col[:, :], 1 - SLOPE, None, ALU.mult))
                pool.tensor_scalar(s2_col[:, :], s_col[:, :], SLOPE, None,
                                   ALU.mult).then_inc(cols_made, 1)
                pool.wait_ge(cols_made, layer + 1)

            def diagonal(layer, g):
                n = layer * G + g
                if n >= 2:
                    pool.wait_ge(scored, T * (n - 1))
                pool.tensor_tensor(
                    s_row[:, n % 2, :].rearrange("p (k q) -> p k q", k=GT),
                    ident[:, :].unsqueeze(1).to_broadcast([P, GT, P]),
                    s8_col[:, g * GT:(g + 1) * GT].unsqueeze(2).to_broadcast([P, GT, P]),
                    ALU.mult).then_inc(diag_made, 1)

            def guard(layer, g):
                n = layer * G + g
                cols = slice(g * GT, (g + 1) * GT)
                pool.wait_ge(lowest_made, n + 1)
                mine(pool.tensor_scalar(empty[:, n % 2, :], lowest[:, :], 0.5, None, ALU.is_gt))
                mine(pool.tensor_scalar(mz[:, 0, :], lowest[:, :], -1.0 / SHRINK, None, ALU.mult))
                mine(pool.tensor_tensor(mz[:, 1, :], mz[:, 0, :], s_col[:, cols], ALU.add))
                mine(pool.tensor_scalar(mz[:, 2, :], mz[:, 1, :], 0.0, SLOPE, ALU.min, ALU.mult))
                mine(pool.tensor_scalar(mz[:, 3, :], mz[:, 1, :], 0.0, None, ALU.max))
                mine(pool.tensor_tensor(mz[:, 4, :], mz[:, 2, :], mz[:, 3, :], ALU.add))
                mine(pool.tensor_tensor(mz[:, 5, :], s2_col[:, cols], mz[:, 4, :], ALU.subtract))
                if n >= 1:
                    pool.wait_ge(rows_done, n)
                mine(pool.tensor_copy(u_parts[:, :, 0], mz[:, 5, :]))
                mine(pool.tensor_tensor(mz[:, 0, :], mz[:, 5, :], u_parts[:, :, 0], ALU.subtract))
                mine(pool.tensor_copy(u_parts[:, :, 1], mz[:, 0, :]))
                mine(pool.tensor_tensor(mz[:, 1, :], mz[:, 0, :], u_parts[:, :, 1], ALU.subtract))
                pool.tensor_copy(u_parts[:, :, 2], mz[:, 1, :]).then_inc(parts_made, 1)
                pool.wait_ge(parts_made, n + 1)

            def wide(column):
                return column.unsqueeze(2).to_broadcast([P, GT, F])

            def finish(layer, g):
                n = layer * G + g
                here = nodes[:, g * GT:(g + 1) * GT, :]
                pool.wait_ge(attended_made, n + 1)
                if n == 0:
                    pool.wait_ge(nodes_in, 32)
                pool.wait_ge(sum_kept, layer + 1)
                mine(pool.tensor_tensor(
                    tmp_a[:, :, :], value_sum[:, 0:F].unsqueeze(1).to_broadcast([P, GT, F]),
                    wide(empty[:, n % 2, :]), ALU.mult))
                mine(pool.tensor_tensor(tmp_b[:, :, :], attended[:, :, 0:F], tmp_a[:, :, :], ALU.add))
                pool.wait_ge(den_made, 2 * (n + 1))
                mine(pool.tensor_tensor(tmp_a[:, :, :], tmp_b[:, :, :], wide(dens[:, 1, :]), ALU.mult))
                h, other = tmp_a, tmp_b
                if layer == 0:
                    mine(pool.tensor_tensor(tmp_b[:, :, :], tmp_a[:, :, :], here, ALU.add))
                    h, other = tmp_b, tmp_a
                pool.tensor_scalar(other[:, :, :], h[:, :, :], 0.0, None, ALU.min).then_inc(neg_made, 1)
                mine(pool.tensor_scalar(h[:, :, :], h[:, :, :], 0.0, -1.0, ALU.max, ALU.add))
                pool.wait_ge(neg_exped, n + 1)
                mine(pool.tensor_tensor(h[:, :, :], h[:, :, :], other[:, :, :], ALU.add))
                pool.tensor_tensor(here, here, h[:, :, :], ALU.add).then_inc(y_made, 1)
                pool.wait_ge(mean_made, n + 1)
                mine(pool.tensor_scalar(stats[:, 1, :], stats[:, 0, :], 1.0 / F, None, ALU.mult))
                mine(pool.tensor_tensor(here, here, wide(stats[:, 1, :]), ALU.subtract))
                pool.tensor_tensor(tmp_a[:, :, :], here, here, ALU.mult).then_inc(square_made, 1)
                pool.wait_ge(var_made, n + 1)
                mine(pool.tensor_scalar(stats[:, 3, :], stats[:, 2, :], 1.0 / F, EPS, ALU.mult, ALU.add))
                mine(pool.tensor_tensor(stats[:, 1, :], stats[:, 3, :], half_neg[:, :], ALU.pow))
                pool.tensor_tensor(here, here, wide(stats[:, 1, :]), ALU.mult).then_inc(normed, 1)

            for layer in range(2):
                columns(layer)
                diagonal(layer, 0)
                guard(layer, 0)
                for g in range(G):
                    if g + 1 < G:
                        diagonal(layer, g + 1)
                    if g > 0:
                        finish(layer, g - 1)
                    if g + 1 < G:
                        guard(layer, g + 1)
                finish(layer, G - 1)

        @block.scalar
        def _(act):
            def mask_chunk(layer, t, k, half):
                act.wait_ge(chunk_in[half], 16 * T * layer + 16 * (t + 1))
                nc.scalar.activation(absent[:, k, half * H:(half + 1) * H], edges[:, half, :],
                                     ACT.Relu, bias=1.0, scale=-1.0).then_inc(chunk_masked, 1)

            def exp_step(layer, g, jt, slot, wait_used):
                act.wait_ge(scored, (layer * G + g) * T + jt + 1)
                step_used = (layer * G + g) * T + jt - 1
                if wait_used:
                    act.wait_ge(used, step_used)
                nc.scalar.copy(values_now[:, slot, :],
                               values[:, bass.ds(jt, 1), :].rearrange("p a f -> p (a f)"))
                nc.scalar.activation(probs[:, slot, :], work[slot][:, :], ACT.Exp,
                                     bias=d_col[:, bass.ds(jt, 1)]).then_inc(exped, 1)

            def keep_node(layer):
                for c in range(T // 4):
                    tiles = slice(4 * c, 4 * c + 4)
                    act.wait_ge(node_done, 8 * layer + c + 1)
                    if layer == 0:
                        nc.scalar.copy(d_col[:, tiles], acc[:, c % 2, 0:4])
                        nc.scalar.copy(s_col[:, tiles], acc[:, c % 2, 4:8])
                    else:
                        got = acc[:, c % 2, 0:4 * (F + 2)].rearrange("p (t f) -> p t f", t=4)
                        nc.scalar.copy(values[:, tiles, 0:F], got[:, :, 0:F])
                        nc.scalar.copy(d_col[:, tiles], got[:, :, F])
                        nc.scalar.copy(s_col[:, tiles], got[:, :, F + 1])
                    nc.scalar.mul(d_row[:, c * BANK:(c + 1) * BANK], work[c % 2][:, 0:BANK],
                                  -SHRINK).then_inc(node_kept, 1)

            def keep_spread(n):
                act.wait_ge(spread_done, n + 1)
                nc.scalar.copy(s_row[:, n % 2, :], misc[:, :, :].rearrange("p a b -> p (a b)")
                               ).then_inc(spread_kept, 1)

            def keep_rows(n):
                act.wait_ge(rows_done, n + 1)
                at = 32 * (n % 2)
                nc.scalar.copy(u_rows[at:at + 3, :], misc[0:3, :, :].rearrange("p a b -> p (a b)")
                               ).then_inc(rows_kept, 1)

            def keep_sum(layer):
                act.wait_ge(sum_done, layer + 1)
                nc.scalar.copy(value_sum[:, :], misc[:, 0, 0:VW]).then_inc(sum_kept, 1)

            def keep_acc(n):
                act.wait_ge(used, T * (n + 1))
                if n > 0:
                    act.wait_ge(normed, n)
                nc.scalar.copy(acc_sb, acc[0:VW, :, :].rearrange("p a b -> p (a b)")
                               ).then_inc(acc_kept, 1)

            def keep_attended(n):
                act.wait_ge(acc_turned, n + 1)
                nc.scalar.copy(attended[:, :, :].rearrange("p (a k) f -> p a (k f)", a=2),
                               misc[:, :, 0:4 * VW]).then_inc(attended_made, 1)

            def exp_neg(layer, g):
                n = layer * G + g
                act.wait_ge(neg_made, n + 1)
                it = tmp_a if layer == 0 else tmp_b
                nc.scalar.activation(it[:, :, :], it[:, :, :], ACT.Exp).then_inc(neg_exped, 1)

            def group(layer, g):
                n = layer * G + g
                nxt = n + 1
                incoming = nxt < 2 * G
                nlayer, ng = nxt // G, nxt % G
                if incoming and nxt >= 2:
                    act.wait_ge(filled, T * (nxt - 1))

                def six(q, first):
                    for i in range(SIX):
                        exp_step(layer, g, q * SIX + i, i % 2, n > 0 or not first or i > 1)
                        if first and i == 0 and g > 0:
                            keep_acc(n - 1)
                        if first and i == 4 and g > 0:
                            keep_attended(n - 1)
                        if incoming and i < 4:
                            k = q * 2 + i // 2
                            mask_chunk(nlayer, k + ng * GT, k + (nxt % 2) * GT, i % 2)

                six(0, True)
                with act.Fori(1, GT // 2) as q:
                    six(q, False)
                if g > 0:
                    exp_neg(layer, g - 1)
                if g + 1 < G:
                    keep_spread(n + 1)
                with act.Fori(LEAD // 2, T // 2) as q:
                    for i in range(2):
                        exp_step(layer, g, q * 2 + i, i, True)
                if g + 1 < G:
                    keep_rows(n + 1)

            keep_node(0)
            with act.Fori(0, GT) as k:
                for half in range(2):
                    mask_chunk(0, k, k, half)
            for layer in range(2):
                if layer == 1:
                    keep_node(1)
                keep_sum(layer)
                keep_spread(layer * G)
                keep_rows(layer * G)
                for g in range(G):
                    group(layer, g)
                keep_acc(layer * G + G - 1)
                keep_attended(layer * G + G - 1)
                exp_neg(layer, G - 1)

        @block.vector
        def _(dve):
            dve.memset(ones[:, :], 1.0).then_inc(ones_made, 1)
            dve.memset(pick[:, :, :], 0.0).then_inc(ones_made, 1)
            dve.memset(u_rows[:, :], 0.0).then_inc(ones_made, 1)
            dve.wait_ge(ones_made, 3)
            dve.memset(pick[0:3, 0, :], 1.0).then_inc(ones_made, 1)
            dve.memset(pick[32:35, 1, :], 1.0).then_inc(ones_made, 1)
            dve.wait_ge(weights_in, 16 * 5)
            for layer in range(2):
                dve.tensor_scalar(a_rep[:, layer, :], ones[0:F, :], a_sb[:, layer, 1:2], None,
                                  ALU.mult).then_inc(reps_made, 1)
            dve.wait_ge(weights_done, 1)
            dve.tensor_copy(w_rep[:, 0, :], misc[0:F, 0, 0:P])
            dve.tensor_copy(w_rep[:, 1, :], misc[0:F, 0, P:2 * P])
            dve.tensor_copy(into1[:, F:F + 1], misc[0:F, 0, P:P + 1])
            dve.tensor_copy(into1[:, F + 1:F + 2], misc[0:F, 0, 2 * P + 1:2 * P + 2])
            dve.tensor_copy(w_src[:, 0:1], misc[0:F, 0, 2 * P:2 * P + 1]).then_inc(weights_kept, 1)
            dve.wait_ge(nodes_in, 32)
            dve.memset(values[:, :, F:F + 1], 1.0).then_inc(ones_made, 1)

            def lowest_of_chunk(layer, g, k, half):
                n = layer * G + g
                c = 2 * (n * GT + k) + half
                dve.wait_ge(chunk_masked, c + 1)
                if c > 0:
                    dve.wait_ge(row_low, c)
                dve.tensor_tensor_reduce(
                    out=unused[:, :], in0=absent[:, (n % 2) * GT + k, half * H:(half + 1) * H],
                    in1=d_row[:, half * H:(half + 1) * H], scale=1.0, scalar=BIG,
                    op0=ALU.add, op1=ALU.min,
                    accum_out=low[:, half, k:k + 1]).then_inc(row_low, 1)

            def lowest_of_group(layer, g):
                n = layer * G + g
                dve.wait_ge(row_low, 2 * GT * (n + 1))
                dve.tensor_tensor(lowest[:, :], low[:, 0, :], low[:, 1, :],
                                  ALU.min).then_inc(lowest_made, 1)

            def score_step(layer, g, jt):
                n = layer * G + g
                step = n * T + jt
                dve.wait_ge(filled, step + 1)
                dve.scalar_tensor_tensor(out=work[jt % 2][:, :], in0=s_row[:, n % 2, :],
                                         scalar=nd8_col[:, jt:jt + 1], in1=work[jt % 2][:, :],
                                         op0=ALU.max, op1=ALU.add).then_inc(scored, 1)

            def denominator(layer, g):
                n = layer * G + g
                dve.wait_ge(attended_made, n + 1)
                dve.scalar_tensor_tensor(out=dens[:, 0, :], in0=empty[:, n % 2, :], scalar=float(N),
                                         in1=attended[:, :, F], op0=ALU.mult,
                                         op1=ALU.add).then_inc(den_made, 1)
                dve.wait_ge(den_made, 2 * n + 1)
                dve.reciprocal(dens[:, 1, :], dens[:, 0, :]).then_inc(den_made, 1)

            def row_sums(layer, g, second):
                n = layer * G + g
                if not second:
                    dve.wait_ge(y_made, n + 1)
                    dve.tensor_reduce(stats[:, 0, :], nodes[:, g * GT:(g + 1) * GT, :], AX.X,
                                      ALU.add).then_inc(mean_made, 1)
                else:
                    dve.wait_ge(square_made, n + 1)
                    dve.tensor_reduce(stats[:, 2, :], tmp_a[:, :, :], AX.X,
                                      ALU.add).then_inc(var_made, 1)

            def turn_nodes():
                for c in range(T // 4):
                    dve.wait_ge(turned_done, c + 1)
                    dve.tensor_copy(turned[:, c % 2, :],
                                    misc[0:F, c % 2, :]).then_inc(turned_kept, 1)

            for layer in range(2):
                if layer == 1:
                    turn_nodes()
                dve.wait_ge(node_kept, 8 * (layer + 1))
                for k in range(GT):
                    for half in range(2):
                        lowest_of_chunk(layer, 0, k, half)
                lowest_of_group(layer, 0)
                dve.wait_ge(cols_made, layer + 1)
                for g in range(G):
                    dve.wait_ge(spread_kept, layer * G + g + 1)
                    for jt in range(T):
                        score_step(layer, g, jt)
                        if g > 0 and jt == 6:
                            denominator(layer, g - 1)
                        if g > 0 and jt == 27:
                            row_sums(layer, g - 1, False)
                        if g > 0 and jt == 30:
                            row_sums(layer, g - 1, True)
                        i = jt - 2
                        if g + 1 < G and 0 <= i < LEAD and i % 3 < 2:
                            lowest_of_chunk(layer, g + 1, i // 3, i % 3)
                        if g + 1 < G and i == LEAD:
                            lowest_of_group(layer, g + 1)
                denominator(layer, G - 1)
                row_sums(layer, G - 1, False)
                row_sums(layer, G - 1, True)

        @block.tensor
        def _(pe):
            pe.wait_ge(ones_made, 5)
            pe.wait_ge(weights_in, 16 * 5)
            pe.wait_ge(reps_made, 2)
            pe.matmul(misc[0:F, 0, 0:P], w0T_sb, a_rep[:, 0, :], start=True, stop=True)
            pe.matmul(misc[0:F, 0, P:2 * P], w1_sb, a_rep[:, 1, :], start=True, stop=True)
            pe.matmul(misc[0:F, 0, 2 * P:2 * P + 1], w0T_sb, a_sb[:, 0, 0:1],
                      start=True, stop=True)
            pe.matmul(misc[0:F, 0, 2 * P + 1:2 * P + 2], w1_sb, a_sb[:, 1, 0:1],
                      start=True, stop=True).then_inc(weights_done, 1)
            pe.wait_ge(weights_kept, 1)
            pe.wait_ge(columns_in, 32)

            def node0():
                for c in range(T // 4):
                    if c >= 2:
                        pe.wait_ge(node_kept, c - 1)
                    pe.matmul(work[c % 2][:, 0:BANK], w_rep[:, 0, :],
                              eT_sb[:, c * BANK:(c + 1) * BANK], start=True, stop=True)
                    for i in range(4):
                        t = 4 * c + i
                        pe.matmul(acc[:, c % 2, i:i + 1], eT_sb[:, t * P:(t + 1) * P],
                                  w_rep[:, 0, 0:1], start=True, stop=True)
                        last = pe.matmul(acc[:, c % 2, 4 + i:5 + i], xT_sb[:, t * P:(t + 1) * P],
                                         w_src[:, 0:1], start=True, stop=True)
                    last.then_inc(node_done, 1)

            def node1():
                pe.wait_ge(consts_made, 1)
                pe.wait_ge(attended_made, G)
                for c in range(T // 4):
                    pe.wait_ge(normed, c // 2 + 1)
                    if c >= 2:
                        pe.wait_ge(turned_kept, c - 1)
                    for i in range(4):
                        last = pe.transpose(misc[0:F, c % 2, i * P:(i + 1) * P],
                                            nodes[:, 4 * c + i, :], ident[:, :])
                    last.then_inc(turned_done, 1)
                    pe.wait_ge(turned_kept, c + 1)
                    if c >= 2:
                        pe.wait_ge(node_kept, 8 + c - 1)
                    pe.matmul(work[c % 2][:, 0:BANK], w_rep[:, 1, :], turned[:, c % 2, :],
                              start=True, stop=True)
                    for i in range(4):
                        last = pe.matmul(acc[:, c % 2, i * (F + 2):(i + 1) * (F + 2)],
                                         turned[:, c % 2, i * P:(i + 1) * P], into1[:, :],
                                         start=True, stop=True)
                    last.then_inc(node_done, 1)

            def sum_values(layer):
                pe.wait_ge(node_kept, 8 * (layer + 1))
                pe.wait_ge(ones_made, 6)
                for t in range(T):
                    last = pe.matmul(misc[:, 0, 0:VW], ones[:, :], values[:, t, :],
                                     start=(t == 0), stop=(t == T - 1))
                last.then_inc(sum_done, 1)
                pe.wait_ge(sum_kept, layer + 1)

            def spread(n):
                pe.wait_ge(diag_made, n + 1)
                if n % G >= 2:
                    pe.wait_ge(attended_made, n - 1)
                for b in range(2):
                    last = pe.matmul(misc[:, b, :], ones[:, :],
                                     s_row[:, n % 2, b * BANK:(b + 1) * BANK],
                                     start=True, stop=True)
                last.then_inc(spread_done, 1)

            def rows(n):
                pe.wait_ge(parts_made, n + 1)
                pe.wait_ge(spread_kept, n + 1)
                for k in range(GT):
                    last = pe.matmul(misc[0:3, k // 4, (k % 4) * P:(k % 4 + 1) * P],
                                     u_parts[:, k, :], ident_b[:, :], start=True, stop=True)
                last.then_inc(rows_done, 1)
                pe.wait_ge(rows_kept, n + 1)

            def fill(n, jt, slot, fresh):
                if not fresh:
                    pe.wait_ge(exped, n * T + jt - 1)
                for b in range(2):
                    cols = slice(b * BANK, (b + 1) * BANK)
                    pe.matmul(work[slot][:, cols], pick[:, n % 2, :], u_rows[:, cols],
                              start=True, stop=False)
                    for k in range(4 * b, 4 * b + 4):
                        last = pe.matmul(work[slot][:, k * P:(k + 1) * P],
                                         absent[:, (n % 2) * GT + k, bass.ds(jt * P, P)],
                                         minus_big[:, :], start=False, stop=(k % 4 == 3))
                last.then_inc(filled, 1)

            def use(n, jt, slot, first):
                pe.wait_ge(exped, n * T + jt + 1)
                for b in range(2):
                    last = pe.matmul(acc[0:VW, b, :], values_now[:, slot, :],
                                     probs[:, slot, b * BANK:(b + 1) * BANK],
                                     start=first, stop=False, skip_group_check=True)
                last.then_inc(used, 1)

            def turn_acc(n):
                pe.wait_ge(acc_kept, n + 1)
                for k in range(GT):
                    last = pe.transpose(misc[:, k // 4, (k % 4) * VW:(k % 4 + 1) * VW],
                                        acc_sb[:, k * P:(k + 1) * P], ident[0:VW, 0:VW])
                last.then_inc(acc_turned, 1)

            node0()
            for layer in range(2):
                if layer == 1:
                    node1()
                sum_values(layer)
                spread(layer * G)
                rows(layer * G)
                for g in range(G):
                    n = layer * G + g
                    for jt in range(2):
                        fill(n, jt, jt, n == 0)
                        if g > 0:
                            use(n - 1, T - 2 + jt, jt, False)
                    if g > 0:
                        pe.wait_ge(acc_kept, n)
                    for jt in range(2, 4):
                        fill(n, jt, jt % 2, False)
                        use(n, jt - 2, jt % 2, jt == 2)
                    if g > 0:
                        turn_acc(n - 1)
                    with pe.Fori(2, LEAD // 2) as q:
                        for i in range(2):
                            fill(n, q * 2 + i, i, False)
                            use(n, q * 2 + i - 2, i, False)
                    if g + 1 < G:
                        spread(n + 1)
                    with pe.Fori(LEAD // 2, T // 2) as q:
                        for i in range(2):
                            fill(n, q * 2 + i, i, False)
                            use(n, q * 2 + i - 2, i, False)
                    if g + 1 < G:
                        rows(n + 1)
                for jt in range(T - 2, T):
                    use(layer * G + G - 1, jt, jt % 2, False)
                turn_acc(layer * G + G - 1)


def kernel(x, adj, L0_gnn_entity_embs, L0_gnn_W, L0_gnn_a, L1_gnn_W, L1_gnn_a):
    import numpy as _np
    import concourse.bacc as _bacc
    from concourse import mybir as _mybir
    from concourse.bass_utils import run_bass_kernel_spmd as _run

    nc = _bacc.Bacc("TRN2", target_bir_lowering=False, num_devices=1)
    x, e = _np.asarray(x), _np.asarray(L0_gnn_entity_embs)
    w0, w1 = _np.asarray(L0_gnn_W), _np.asarray(L1_gnn_W)
    given = {
        "x": x, "adj": _np.asarray(adj), "e": e,
        "eT": e.T, "xT": x.T,
        "w0T": w0.T, "a0": _np.asarray(L0_gnn_a).reshape(2, -1).T,
        "w1": w1, "w1T": w1.T, "a1": _np.asarray(L1_gnn_a).reshape(2, -1).T,
    }
    arrays, args = {}, []
    for name, a in given.items():
        a = _np.ascontiguousarray(a)
        arrays[f"in_{name}_dram"] = a
        args.append(nc.dram_tensor(f"in_{name}_dram", a.shape, _mybir.dt.from_np(a.dtype),
                                   kind="ExternalInput").ap())
    out = nc.dram_tensor("out_dram", x.shape, _mybir.dt.from_np(x.dtype), kind="ExternalOutput").ap()
    two_attention_layers(nc, *args, out)
    return _run(nc, [arrays], core_ids=[0]).results[0]["out_dram"]
```

```python
from contextlib import ExitStack

import concourse.bass as bass
from concourse import mybir

ALU = mybir.AluOpType
ACT = mybir.ActivationFunctionType
AX = mybir.AxisListType
F32 = mybir.dt.float32
BF16 = mybir.dt.bfloat16
I32 = mybir.dt.int32
U8 = mybir.dt.uint8

P = 128
SLOPE = 0.2
EPS = 1e-5
SHRINK = 2.0 ** -40
BIG = 2.0 ** 60


def two_attention_layers(nc, adj, eT, xT, w0T, a0, w1, w1T, a1, out):
    F, N = xT.shape
    T = N // P
    GT = 8
    G = T // GT
    GW = GT * P
    C = -(-N // 3)
    CHUNKS = [(c, min(c + C, N)) for c in range(0, N, C)]
    BANK = 512
    VW = F + 1
    SIX = 6
    LEAD = 3 * GT
    TURN_AT = (6, 10, 14, 18, 22, 26)

    with ExitStack() as ctx:
        def sb(name, shape, dt):
            return ctx.enter_context(nc.sbuf_tensor(name, shape, dt))

        def sem(name):
            return ctx.enter_context(nc.semaphore(name))

        absent = sb("absent", [P, 2 * GT, N], BF16)
        edges = sb("edges", [P, 3, C], I32)
        d_row = sb("d_row", [P, N], F32)
        s_row = sb("s_row", [P, 2, GW], F32)
        probs = sb("probs", [P, 2, GW], F32)
        nodes = sb("nodes", [P, T, VW], F32)
        entities = sb("entities", [P, T, VW], F32)
        values = [entities, nodes]
        results = [nodes, entities]
        values_now = sb("values_now", [P, 2, VW], F32)
        unused = sb("unused", [P, C + C // 8], U8)
        u_rows = sb("u_rows", [P, GW], BF16)
        attended = sb("attended", [P, GT, VW], F32)
        tmp = sb("tmp", [P, 2, GT, F], F32)
        tmp_a, tmp_b = tmp[:, 0, :, :], tmp[:, 1, :, :]
        acc_sb = tmp[0:VW, :, :, :].rearrange("p a k f -> p (a k f)")
        ident = sb("ident", [P, P], F32)
        ident_b = sb("ident_b", [P, P], BF16)
        minus_big = sb("minus_big", [P, P], BF16)
        ones = sb("ones", [P, P], F32)
        pick = sb("pick", [P, P], BF16)
        value_sum = sb("value_sum", [P, VW], F32)
        d_col = sb("d_col", [P, 2, T], F32)
        nd8_col = sb("nd8_col", [P, 2, T], F32)
        s_col = sb("s_col", [P, 2, T], F32)
        s8_col = sb("s8_col", [P, 2, T], F32)
        low = sb("low", [P, 4, GT], F32)
        lowest = sb("lowest", [P, GT], F32)
        empty = sb("empty", [P, 2, GT], F32)
        guards = sb("guards", [P, 4, GT], F32)
        u_parts = sb("u_parts", [P, GT, 3], BF16)
        dens = sb("dens", [P, 2, GT], F32)
        stats = sb("stats", [P, 4, GT], F32)
        half_neg = sb("half_neg", [P, GT], F32)
        w0T_sb, w1_sb, w1T_sb = tmp_b[0:F, 0, :], tmp_b[0:F, 1, :], tmp_b[0:F, 3, :]
        a_sb = tmp_b[0:F, 2, 0:4].rearrange("f (l c) -> f l c", l=2)
        a_rep = tmp_a[0:F, 0:4, :].rearrange("f (l h) c -> f l (h c)", l=2)
        sum_rep = tmp_a[0:VW, 0:2, :].rearrange("f a b -> f (a b)")
        w_rep = [tmp_b[0:F, 4:6, :].rearrange("f a b -> f (a b)"),
                 sb("w_rep", [F, P], F32)[:, :]]
        w_cols = sb("w_cols", [F, 2], F32)
        w_wide = sb("w_wide", [F, 2, VW], F32)
        turner = sb("turner", [VW, VW], F32)

        work = [ctx.enter_context(nc.psum_tensor(f"work{i}", [P, GW], F32)) for i in range(2)]
        acc = ctx.enter_context(nc.psum_tensor("acc", [P, 2, BANK], F32))
        misc = ctx.enter_context(nc.psum_tensor("misc", [P, 2, BANK], F32))
        eT_sb = absent[0:F, GT:GT + 2, :].rearrange("p a b -> p (a b)").bitcast(F32)
        xT_sb = absent[0:F, GT + 2:GT + 4, :].rearrange("p a b -> p (a b)").bitcast(F32)
        spare = probs[:, 0, :].bitcast(U8).rearrange("p (s c) -> p s c", s=2)

        weights_in = sem("weights_in")
        eT_in = sem("eT_in")
        xT_in = sem("xT_in")
        chunk_in = [sem(f"chunk_in{i}") for i in range(3)]
        chunk_masked = sem("chunk_masked")
        consts_made = sem("consts_made")
        ones_made = sem("ones_made")
        reps_made = sem("reps_made")
        weights_done = sem("weights_done")
        weights_kept = sem("weights_kept")
        row_turner_made = sem("row_turner_made")
        turned_done = sem("turned_done")
        turned_kept = sem("turned_kept")
        node_done = sem("node_done")
        node_kept = sem("node_kept")
        sum_col_done = sem("sum_col_done")
        sum_rep_made = sem("sum_rep_made")
        sum_done = sem("sum_done")
        sum_kept = sem("sum_kept")
        cols_made = sem("cols_made")
        row_low = sem("row_low")
        lowest_made = sem("lowest_made")
        pool_step = sem("pool_step")
        parts_made = sem("parts_made")
        diag_made = sem("diag_made")
        spread_done = sem("spread_done")
        spread_kept = sem("spread_kept")
        rows_done = sem("rows_done")
        rows_kept = sem("rows_kept")
        filled = sem("filled")
        scored = sem("scored")
        exped = sem("exped")
        used = sem("used")
        acc_kept = sem("acc_kept")
        acc_turned = sem("acc_turned")
        attended_made = sem("attended_made")
        den_made = sem("den_made")
        neg_made = sem("neg_made")
        neg_exped = sem("neg_exped")
        y_made = sem("y_made")
        tiles_done = sem("tiles_done")
        tiles_kept = sem("tiles_kept")
        empty_made = sem("empty_made")
        guard_step = sem("guard_step")
        mean_made = sem("mean_made")
        square_made = sem("square_made")
        finish_step = sem("finish_step")
        spread_var_made = sem("spread_var_made")
        last_scale_made = sem("last_scale_made")
        var_made = sem("var_made")
        normed = sem("normed")
        stored = sem("stored")

        block = ctx.enter_context(nc.Block())

        def tiles_place(i):
            return (acc, misc)[i // 2 % 2][:, i % 2, 0:4 * VW].rearrange("p (t f) -> p t f", t=4)

        def turned_place(c):
            return misc[0:F, 0 if c < 6 else c - 6, :]

        def turned_sb(c):
            if c < 6:
                return d_row[0:F, c * BANK:(c + 1) * BANK]
            return s_row[0:F, 1, (c - 6) * BANK:(c - 5) * BANK]

        def node1_places(c):
            if c < 6:
                return misc[:, 1, :], misc[:, 0, 0:8]
            return work[0][:, (c - 6) * BANK:(c - 5) * BANK], acc[:, c - 6, 0:8]

        def by_tile(a):
            return a.rearrange("(t p) f -> p t f", p=P)

        @block.sync
        def _(sp):
            for to, frm in ((w0T_sb, w0T), (a_sb[:, 0, :], a0), (w1_sb, w1), (a_sb[:, 1, :], a1),
                            (w1T_sb, w1T)):
                sp.dma_start(to, frm).then_inc(weights_in, 16)
            sp.dma_start(eT_sb, eT).then_inc(eT_in, 16)

            def load_tile(layer, t, first):
                for c, (a, b) in enumerate(CHUNKS):
                    if not first:
                        sp.wait_ge(chunk_masked, 3 * T * layer + 3 * t + c - 2)
                    sp.dma_start(edges[:, c, 0:b - a], adj[bass.ds(t * P, P), a:b]
                                 ).then_inc(chunk_in[c], 16)

            load_tile(0, 0, True)
            sp.dma_start(xT_sb, xT).then_inc(xT_in, 16)
            with sp.Fori(1, T) as t:
                load_tile(0, t, False)
            with sp.Fori(0, T) as t:
                load_tile(1, t, False)
            for g in range(G):
                sp.wait_ge(normed, G + g + 1)
                sp.dma_start(by_tile(out)[:, g * GT:(g + 1) * GT, :],
                             results[1][:, g * GT:(g + 1) * GT, 0:F]).then_inc(stored, 16)
            sp.wait_ge(stored, 16 * G)

        @block.gpsimd
        def _(pool):
            steps = [0]

            def mine(ins):
                steps[0] += 1
                ins.then_inc(pool_step, 1)
                pool.wait_ge(pool_step, steps[0])

            mine(pool.memset(ident[:, :], 0.0))
            mine(pool.affine_select(out=ident[:, :], in_=ident[:, :], compare_op=ALU.not_equal,
                                    fill=1.0, base=0, pattern=[[-1, P]], channel_multiplier=1))
            mine(pool.tensor_copy(ident_b[:, :], ident[:, :]))
            mine(pool.tensor_scalar(minus_big[:, :], ident[:, :], -BIG, None, ALU.mult))
            pool.memset(half_neg[:, :], -0.5).then_inc(consts_made, 1)

            def columns(layer):
                if layer == 0:
                    pool.wait_ge(tiles_kept, 16)
                else:
                    pool.wait_ge(node_kept, 8 + 9)
                mine(pool.tensor_scalar(s8_col[:, layer, :], s_col[:, layer, :], 1 - SLOPE, None,
                                        ALU.mult))
                pool.tensor_scalar(nd8_col[:, layer, :], d_col[:, layer, :], -(1 - SLOPE), None,
                                   ALU.mult).then_inc(cols_made, 1)

            def diagonal(layer, g):
                n = layer * G + g
                if n >= 2:
                    pool.wait_ge(scored, T * (n - 1))
                pool.tensor_tensor(
                    s_row[:, n % 2, :].rearrange("p (k q) -> p k q", k=GT),
                    ident[:, :].unsqueeze(1).to_broadcast([P, GT, P]),
                    s8_col[:, layer, g * GT:(g + 1) * GT].unsqueeze(2).to_broadcast([P, GT, P]),
                    ALU.mult).then_inc(diag_made, 1)

            def wide(column):
                return column.unsqueeze(2).to_broadcast([P, GT, F])

            def row_sums(rows, stat):
                width = F // 2
                while width > 1:
                    mine(pool.tensor_tensor(tmp_a[:, :, 0:width], rows[:, :, 0:width],
                                            rows[:, :, width:2 * width], ALU.add))
                    rows, width = tmp_a, width // 2
                mine(pool.tensor_tensor(stats[:, stat, :], rows[:, :, 0], rows[:, :, 1], ALU.add))

            def finish(layer, g):
                n = layer * G + g
                here = nodes[:, g * GT:(g + 1) * GT, 0:F]
                to = results[layer][:, g * GT:(g + 1) * GT, 0:F]
                pool.wait_ge(attended_made, n + 1)
                pool.wait_ge(sum_kept, layer + 1)
                mine(pool.tensor_tensor(
                    tmp_a[:, :, :], value_sum[:, 0:F].unsqueeze(1).to_broadcast([P, GT, F]),
                    wide(empty[:, n % 2, :]), ALU.mult))
                mine(pool.tensor_tensor(tmp_b[:, :, :], attended[:, :, 0:F], tmp_a[:, :, :], ALU.add))
                pool.wait_ge(den_made, 2 * (n + 1))
                mine(pool.tensor_tensor(tmp_a[:, :, :], tmp_b[:, :, :], wide(dens[:, 1, :]), ALU.mult))
                h, other = tmp_a, tmp_b
                if layer == 0:
                    mine(pool.tensor_tensor(tmp_b[:, :, :], tmp_a[:, :, :], here, ALU.add))
                    h, other = tmp_b, tmp_a
                pool.tensor_scalar(other[:, :, :], h[:, :, :], 0.0, None, ALU.min).then_inc(neg_made, 1)
                mine(pool.tensor_scalar(h[:, :, :], h[:, :, :], 0.0, -1.0, ALU.max, ALU.add))
                pool.wait_ge(neg_exped, n + 1)
                mine(pool.tensor_tensor(h[:, :, :], h[:, :, :], other[:, :, :], ALU.add))
                mine(pool.tensor_tensor(to, here, h[:, :, :], ALU.add))
                row_sums(to, 0)
                mine(pool.tensor_scalar(stats[:, 1, :], stats[:, 0, :], 1.0 / F, None, ALU.mult))
                mine(pool.tensor_tensor(to, to, wide(stats[:, 1, :]), ALU.subtract))
                mine(pool.tensor_tensor(tmp_b[:, :, :], to, to, ALU.mult))
                row_sums(tmp_b, 2)
                mine(pool.tensor_scalar(stats[:, 3, :], stats[:, 2, :], 1.0 / F, EPS, ALU.mult, ALU.add))
                mine(pool.tensor_tensor(stats[:, 1, :], stats[:, 3, :], half_neg[:, :], ALU.pow))
                pool.tensor_tensor(to, to, wide(stats[:, 1, :]), ALU.mult).then_inc(normed, 1)

            for layer in range(2):
                columns(layer)
                diagonal(layer, 0)
                for g in range(G):
                    if g + 1 < G:
                        diagonal(layer, g + 1)
                    if g > 0:
                        finish(layer, g - 1)
                pool.wait_ge(spread_var_made, layer + 1)
                pool.tensor_tensor(stats[:, 1, :], stats[:, 3, :], half_neg[:, :],
                                   ALU.pow).then_inc(last_scale_made, 1)

        @block.scalar
        def _(act):
            def mask_chunk(layer, t, k, c):
                a, b = CHUNKS[c]
                act.wait_ge(chunk_in[c], 16 * T * layer + 16 * (t + 1))
                nc.scalar.activation(absent[:, k, a:b], edges[:, c, 0:b - a],
                                     ACT.Relu, bias=1.0, scale=-1.0).then_inc(chunk_masked, 1)

            def exp_step(layer, g, jt, slot, wait_used):
                n = layer * G + g
                act.wait_ge(scored, n * T + jt + 1)
                if wait_used:
                    act.wait_ge(used, n * T + jt - 1)
                nc.scalar.copy(values_now[:, slot, :], values[layer][:, bass.ds(jt, 1), :]
                               .rearrange("p a f -> p (a f)"))
                nc.scalar.activation(probs[:, slot, :], work[slot][:, :], ACT.Exp,
                                     bias=d_col[:, layer, bass.ds(jt, 1)]).then_inc(exped, 1)

            def keep_node1(c):
                tiles = slice(4 * c, 4 * c + 4)
                act.wait_ge(node_done, 8 + c + 1)
                d_all, got = node1_places(c)
                got = got.rearrange("p (t c) -> p t c", t=4)
                ins = nc.scalar.mul(d_row[:, c * BANK:(c + 1) * BANK], d_all, -SHRINK)
                if c >= 6:
                    ins.then_inc(node_kept, 1)
                    return
                nc.scalar.copy(d_col[:, 1, tiles], got[:, :, 0])
                nc.scalar.copy(s_col[:, 1, tiles], got[:, :, 1]).then_inc(node_kept, 1)

            def keep_last_cols():
                act.wait_ge(node_done, 8 + 9)
                for c in (6, 7):
                    tiles = slice(4 * c, 4 * c + 4)
                    got = node1_places(c)[1].rearrange("p (t c) -> p t c", t=4)
                    nc.scalar.copy(d_col[:, 1, tiles], got[:, :, 0])
                    last = nc.scalar.copy(s_col[:, 1, tiles], got[:, :, 1])
                last.then_inc(node_kept, 1)

            def keep_spread(n):
                act.wait_ge(spread_done, n + 1)
                nc.scalar.copy(s_row[:, n % 2, :], misc[:, :, :].rearrange("p a b -> p (a b)")
                               ).then_inc(spread_kept, 1)

            def keep_rows(n):
                act.wait_ge(rows_done, n + 1)
                at = 64 * (n % 2)
                nc.scalar.copy(u_rows[at:at + 3, :], misc[0:3, :, :].rearrange("p a b -> p (a b)")
                               ).then_inc(rows_kept, 1)

            def keep_sum(layer):
                act.wait_ge(sum_done, layer + 1)
                nc.scalar.copy(value_sum[:, :], acc[:, 1, 0:VW]).then_inc(sum_kept, 1)

            def keep_acc(n):
                act.wait_ge(used, T * (n + 1))
                if n > 0:
                    act.wait_ge(normed, n)
                for b in range(2):
                    nc.scalar.copy(acc_sb[:, b * BANK:(b + 1) * BANK],
                                   acc[0:VW, b, :]).then_inc(acc_kept, 1)

            def keep_attended(n):
                act.wait_ge(acc_turned, n + 1)
                nc.scalar.copy(attended[:, :, :].rearrange("p (a k) f -> p a (k f)", a=2),
                               misc[:, :, 0:4 * VW]).then_inc(attended_made, 1)

            def exp_neg(layer, g):
                n = layer * G + g
                act.wait_ge(neg_made, n + 1)
                it = tmp_a if layer == 0 else tmp_b
                nc.scalar.activation(it[:, :, :], it[:, :, :], ACT.Exp).then_inc(neg_exped, 1)

            def group(layer, g):
                n = layer * G + g
                nxt = n + 1
                incoming = nxt < 2 * G
                nlayer, ng = nxt // G, nxt % G
                if incoming and nxt >= 2:
                    act.wait_ge(filled, T * (nxt - 1))

                def six(q, after):
                    for i in range(SIX):
                        exp_step(layer, g, q * SIX + i, i % 2, n > 0 or "start" not in after or i > 1)
                        for task in after.get(i, ()):
                            task()
                        if incoming:
                            k = q * 2 + i // 3
                            mask_chunk(nlayer, k + ng * GT, k + (nxt % 2) * GT, i % 3)

                early = {"start": ()}
                if g > 0:
                    early[0] = (lambda: keep_acc(n - 1),)
                    early[4] = (lambda: keep_attended(n - 1),)
                six(0, early)
                if n == G - 1:
                    after = {at + 2: c for c, at in enumerate(TURN_AT)}
                    for q in range(1, LEAD // SIX):
                        six(q, {i: (lambda c=after[q * SIX + i]: keep_node1(c),)
                                for i in range(SIX) if q * SIX + i in after} |
                            ({3: (lambda: exp_neg(layer, g - 1),)} if q == 1 else {}))
                    for jt in range(LEAD, T):
                        exp_step(layer, g, jt, jt % 2, True)
                        if jt in after:
                            keep_node1(after[jt])
                    return
                later = {}
                if g > 0:
                    later[3] = (lambda: exp_neg(layer, g - 1),)
                if g + 1 < G:
                    later[5] = (lambda: keep_spread(n + 1),)
                six(1, later)
                with act.Fori(2, GT // 2) as q:
                    six(q, {})
                with act.Fori(LEAD // 2, T // 2 - 1) as q:
                    for i in range(2):
                        exp_step(layer, g, q * 2 + i, i, True)
                exp_step(layer, g, T - 2, 0, True)
                if g + 1 < G:
                    keep_rows(n + 1)
                exp_step(layer, g, T - 1, 1, True)

            def keep_tiles(i):
                tiles = slice(i % 8 * 4, i % 8 * 4 + 4)
                to, col = ((entities, d_col), (nodes, s_col))[i // 8]
                act.wait_ge(tiles_done, i + 1)
                nc.scalar.copy(to[:, tiles, 0:F], tiles_place(i)[:, :, 0:F])
                nc.scalar.copy(col[:, 0, tiles], tiles_place(i)[:, :, F]).then_inc(tiles_kept, 1)

            def mask_tile(k):
                for c in range(3):
                    mask_chunk(0, k, k, c)

            mask_tile(0)
            with act.Fori(1, 3) as k:
                mask_tile(k)
            for k in range(3, 7):
                mask_tile(k)
                for i in range(4 * k - 12, 4 * k - 8):
                    keep_tiles(i)
            mask_tile(7)
            act.wait_ge(ones_made, 7)
            for layer in range(2):
                keep_spread(layer * G)
                keep_sum(layer)
                keep_rows(layer * G)
                for g in range(G):
                    group(layer, g)
                keep_acc(layer * G + G - 1)
                keep_attended(layer * G + G - 1)
                exp_neg(layer, G - 1)
                if layer == 0:
                    keep_node1(6)
                    keep_node1(7)
                    keep_last_cols()

        @block.vector
        def _(dve):
            dve.memset(ones[:, :], 1.0).then_inc(ones_made, 1)
            dve.memset(pick[:, :], 0.0).then_inc(ones_made, 1)
            dve.memset(u_rows[:, :], 0.0).then_inc(ones_made, 1)
            dve.wait_ge(ones_made, 3)
            dve.memset(pick[0:3, :], 1.0).then_inc(ones_made, 1)
            dve.memset(pick[64:67, :], 1.0).then_inc(ones_made, 1)
            dve.wait_ge(weights_in, 16 * 5)
            for layer in range(2):
                dve.tensor_scalar(a_rep[:, layer, :], ones[0:F, :], a_sb[:, layer, 1:2], None,
                                  ALU.mult).then_inc(reps_made, 1)
            dve.wait_ge(consts_made, 1)
            for i in range(2):
                dve.tensor_copy(w_wide[:, i, 0:F], ident[0:F, 0:F])
            dve.wait_ge(weights_done, 1)
            for layer in range(2):
                dve.tensor_copy(w_rep[layer], misc[0:F, 0, layer * P:(layer + 1) * P])
            dve.tensor_copy(w_cols[:, 0:1], misc[0:F, 0, P:P + 1])
            dve.tensor_copy(w_cols[:, 1:2], misc[0:F, 0, 2 * P + 1:2 * P + 2])
            dve.tensor_copy(w_wide[:, 0, F:VW], misc[0:F, 0, 0:1])
            dve.tensor_copy(w_wide[:, 1, F:VW],
                            misc[0:F, 0, 2 * P:2 * P + 1]).then_inc(weights_kept, 1)
            dve.tensor_copy(turner[0:F, 0:F], w1T_sb).then_inc(row_turner_made, 1)
            dve.memset(turner[0:F, F:VW], 0.0).then_inc(row_turner_made, 1)
            dve.memset(turner[F:VW, 0:F], 0.0).then_inc(row_turner_made, 1)
            dve.memset(turner[F:VW, F:VW], 1.0).then_inc(row_turner_made, 1)
            dve.memset(entities[:, :, F:VW], 1.0).then_inc(ones_made, 1)
            dve.memset(nodes[:, :, F:VW], 1.0).then_inc(ones_made, 1)

            pieces = [0]

            def lowest_of_piece(n, k, piece, start, end, probs_free=False):
                dve.wait_ge(chunk_masked, 3 * (n * GT + k) + -(-end // C))
                if pieces[0] > probs_free:
                    dve.wait_ge(row_low, pieces[0] - probs_free)
                out = spare[:, pieces[0] % 2, :] if probs_free else unused
                dve.tensor_tensor_reduce(
                    out=out[:, 0:end - start], in0=absent[:, (n % 2) * GT + k, start:end],
                    in1=d_row[:, start:end], scale=1.0, scalar=BIG, op0=ALU.add, op1=ALU.min,
                    accum_out=low[:, piece, k:k + 1]).then_inc(row_low, 1)
                pieces[0] += 1

            def lowest_of_group(count):
                for piece in range(1, count):
                    dve.wait_ge(row_low, pieces[0])
                    before = low[:, 0, :] if piece == 1 else lowest[:, :]
                    ins = dve.tensor_tensor(lowest[:, :], before, low[:, piece, :], ALU.min)
                    if piece < count - 1:
                        ins.then_inc(row_low, 1)
                        pieces[0] += 1
                ins.then_inc(lowest_made, 1)

            guard_steps = [0]

            def guard(layer, g):
                n = layer * G + g
                s = s_col[:, layer, g * GT:(g + 1) * GT]
                highest, m, u, rest = (guards[:, i, :] for i in range(4))

                def mine(ins):
                    guard_steps[0] += 1
                    ins.then_inc(guard_step, 1)
                    dve.wait_ge(guard_step, guard_steps[0])

                dve.wait_ge(lowest_made, n + 1)
                if n >= 1:
                    dve.wait_ge(rows_done, n)
                dve.tensor_scalar(empty[:, n % 2, :], lowest[:, :], 0.5, None,
                                  ALU.is_gt).then_inc(empty_made, 1)
                mine(dve.scalar_tensor_tensor(out=highest, in0=lowest[:, :], scalar=-1.0 / SHRINK,
                                              in1=s, op0=ALU.mult, op1=ALU.add))
                mine(dve.scalar_tensor_tensor(out=m, in0=highest, scalar=SLOPE, in1=highest,
                                              op0=ALU.mult, op1=ALU.max))
                dve.scalar_tensor_tensor(out=u_parts[:, :, 0], in0=s, scalar=SLOPE, in1=m,
                                         op0=ALU.mult, op1=ALU.subtract)
                mine(dve.scalar_tensor_tensor(out=u, in0=s, scalar=SLOPE, in1=m,
                                              op0=ALU.mult, op1=ALU.subtract))
                dve.tensor_tensor(u_parts[:, :, 1], u, u_parts[:, :, 0], ALU.subtract)
                mine(dve.tensor_tensor(rest, u, u_parts[:, :, 0], ALU.subtract))
                dve.tensor_tensor(u_parts[:, :, 2], rest, u_parts[:, :, 1],
                                  ALU.subtract).then_inc(parts_made, 1)

            def score_step(layer, g, jt):
                n = layer * G + g
                step = n * T + jt
                dve.wait_ge(filled, step + 1)
                dve.scalar_tensor_tensor(out=work[jt % 2][:, :], in0=s_row[:, n % 2, :],
                                         scalar=nd8_col[:, layer, jt:jt + 1], in1=work[jt % 2][:, :],
                                         op0=ALU.max, op1=ALU.add).then_inc(scored, 1)

            def denominator(layer, g):
                n = layer * G + g
                dve.wait_ge(attended_made, n + 1)
                dve.scalar_tensor_tensor(out=dens[:, 0, :], in0=empty[:, n % 2, :], scalar=float(N),
                                         in1=attended[:, :, F], op0=ALU.mult,
                                         op1=ALU.add).then_inc(den_made, 1)
                dve.wait_ge(den_made, 2 * n + 1)
                dve.reciprocal(dens[:, 1, :], dens[:, 0, :]).then_inc(den_made, 1)

            def row_sums(layer, g, second):
                n = layer * G + g
                if not second:
                    dve.wait_ge(y_made, layer + 1)
                    dve.tensor_reduce(stats[:, 0, :], results[layer][:, g * GT:(g + 1) * GT, 0:F], AX.X,
                                      ALU.add).then_inc(mean_made, 1)
                else:
                    dve.wait_ge(square_made, layer + 1)
                    dve.tensor_reduce(stats[:, 2, :], tmp_a[:, :, :], AX.X,
                                      ALU.add).then_inc(var_made, 1)

            def keep_turned(c):
                dve.wait_ge(turned_done, c + 1)
                dve.tensor_copy(turned_sb(c), turned_place(c)).then_inc(turned_kept, 1)

            def spread_sum(layer):
                dve.wait_ge(sum_col_done, layer + 1)
                dve.tensor_scalar(sum_rep, ones[0:VW, :], acc[0:VW, 0, 0:1], None,
                                  ALU.mult).then_inc(sum_rep_made, 1)

            finish_steps = [0]

            def mine(ins):
                finish_steps[0] += 1
                ins.then_inc(finish_step, 1)
                dve.wait_ge(finish_step, finish_steps[0])

            def wide(column, width=F):
                return column.unsqueeze(2).to_broadcast([P, GT, width])

            def finish_last(layer):
                n = layer * G + G - 1
                here = nodes[:, (G - 1) * GT:T, 0:F]
                to = results[layer][:, (G - 1) * GT:T, 0:F]
                all_alike = s_row[:, (n + 1) % 2, 0:GT * F].rearrange("p (k f) -> p k f", k=GT)
                mine(dve.tensor_tensor(
                    all_alike, value_sum[:, 0:F].unsqueeze(1).to_broadcast([P, GT, F]),
                    wide(empty[:, n % 2, :]), ALU.mult))
                denominator(layer, G - 1)
                mine(dve.tensor_tensor(tmp_b[:, :, :], attended[:, :, 0:F], all_alike, ALU.add))
                dve.wait_ge(den_made, 2 * (n + 1))
                mine(dve.tensor_tensor(tmp_a[:, :, :], tmp_b[:, :, :], wide(dens[:, 1, :]), ALU.mult))
                h, other = tmp_a, tmp_b
                if layer == 0:
                    mine(dve.tensor_tensor(tmp_b[:, :, :], tmp_a[:, :, :], here, ALU.add))
                    h, other = tmp_b, tmp_a
                dve.tensor_scalar(other[:, :, :], h[:, :, :], 0.0, None, ALU.min).then_inc(neg_made, 1)
                mine(dve.scalar_tensor_tensor(out=h[:, :, :], in0=h[:, :, :], scalar=0.0, in1=here,
                                              op0=ALU.max, op1=ALU.add))
                dve.wait_ge(neg_exped, n + 1)
                dve.scalar_tensor_tensor(out=to, in0=other[:, :, :], scalar=-1.0, in1=h[:, :, :],
                                         op0=ALU.add, op1=ALU.add).then_inc(y_made, 1)
                row_sums(layer, G - 1, False)
                dve.wait_ge(mean_made, layer + 1)
                mine(dve.tensor_scalar(stats[:, 1, :], stats[:, 0, :], 1.0 / F, None, ALU.mult))
                mine(dve.tensor_tensor(to, to, wide(stats[:, 1, :]), ALU.subtract))
                dve.tensor_tensor(tmp_a[:, :, :], to, to, ALU.mult).then_inc(square_made, 1)
                row_sums(layer, G - 1, True)
                dve.wait_ge(var_made, layer + 1)
                dve.tensor_scalar(stats[:, 3, :], stats[:, 2, :], 1.0 / F, EPS, ALU.mult,
                                  ALU.add).then_inc(spread_var_made, 1)
                dve.wait_ge(last_scale_made, layer + 1)
                dve.tensor_tensor(to, to, wide(stats[:, 1, :]), ALU.mult).then_inc(normed, 1)

            CUTS = [0, C, 5 * BANK, 6 * BANK, N]
            for layer in range(2):
                if layer == 0:
                    for c in range(N // BANK):
                        dve.wait_ge(node_done, c + 1)
                        dve.tensor_scalar(d_row[:, c * BANK:(c + 1) * BANK],
                                          work[c // 2 % 2][:, c % 2 * BANK:(c % 2 + 1) * BANK],
                                          -SHRINK, None, ALU.mult).then_inc(node_kept, 1)
                    dve.wait_ge(node_kept, 8)
                    for k in range(GT):
                        for c, (a, b) in enumerate(CHUNKS):
                            lowest_of_piece(0, k, c, a, b, True)
                        if k == 6:
                            spread_sum(0)
                    lowest_of_group(3)
                    dve.wait_ge(tiles_kept, 16)
                    guard(0, 0)
                dve.wait_ge(cols_made, layer + 1)
                for g in range(G):
                    n = layer * G + g
                    dve.wait_ge(spread_kept, n + 1)
                    for jt in range(T):
                        score_step(layer, g, jt)
                        if g > 0 and jt == 6:
                            denominator(layer, g - 1)
                        if g + 1 < G and 2 <= jt < 2 + LEAD:
                            k, c = divmod(jt - 2, 3)
                            lowest_of_piece(n + 1, k, c, *CHUNKS[c])
                        if g + 1 < G and jt == 2 + LEAD:
                            lowest_of_group(3)
                        if g + 1 < G and jt == 3 + LEAD:
                            guard(layer, g + 1)
                        if n == G - 1:
                            if jt in TURN_AT:
                                keep_turned(TURN_AT.index(jt))
                            if jt == T - 13:
                                dve.wait_ge(node_kept, 8 + 3)
                            if jt == T - 5:
                                dve.wait_ge(node_kept, 8 + 5)
                            if T - 13 <= jt:
                                piece, k = divmod(jt - (T - 13), GT)
                                lowest_of_piece(G, k, piece, CUTS[piece], CUTS[piece + 1])
                if layer == 0:
                    dve.wait_ge(node_kept, 8 + 6)
                    for k in range(5, GT):
                        lowest_of_piece(G, k, 1, CUTS[1], CUTS[2])
                finish_last(layer)
                if layer == 0:
                    keep_turned(6)
                    keep_turned(7)
                    for k in range(GT):
                        lowest_of_piece(G, k, 2, CUTS[2], CUTS[3], True)
                    dve.wait_ge(node_kept, 8 + 8)
                    for k in range(GT):
                        lowest_of_piece(G, k, 3, CUTS[3], CUTS[4], True)
                        if k == 4:
                            spread_sum(1)
                    lowest_of_group(4)
                    guard(1, 0)

        @block.tensor
        def _(pe):
            pe.wait_ge(ones_made, 5)
            pe.wait_ge(weights_in, 16 * 5)
            pe.wait_ge(reps_made, 2)
            for layer, w in ((0, w0T_sb), (1, w1_sb)):
                pe.matmul(misc[0:F, 0, layer * P:(layer + 1) * P], w, a_rep[:, layer, :],
                          start=True, stop=True)
            for layer, w in ((0, w0T_sb), (1, w1_sb)):
                last = pe.matmul(misc[0:F, 0, 2 * P + layer:2 * P + layer + 1], w,
                                 a_sb[:, layer, 0:1], start=True, stop=True)
            last.then_inc(weights_done, 1)
            pe.wait_ge(weights_kept, 1)
            pe.wait_ge(eT_in, 16)

            def entity_rows():
                for c in range(N // BANK):
                    if c >= 4:
                        pe.wait_ge(node_kept, c - 3)
                    pe.matmul(work[c // 2 % 2][:, c % 2 * BANK:(c % 2 + 1) * BANK], w_rep[0],
                              eT_sb[:, c * BANK:(c + 1) * BANK],
                              start=True, stop=True).then_inc(node_done, 1)

            def tiles():
                for i in range(16):
                    if i == 8:
                        pe.wait_ge(xT_in, 16)
                    if i >= 4:
                        pe.wait_ge(tiles_kept, i - 3)
                    for t in range(4):
                        at = (i % 8 * 4 + t) * P
                        last = pe.matmul(tiles_place(i)[:, t, :],
                                         (eT_sb, xT_sb)[i // 8][:, at:at + P],
                                         w_wide[:, i // 8, :], start=True, stop=True)
                    last.then_inc(tiles_done, 1)

            def turn_nodes(c):
                pe.wait_ge(normed, c // 2 + 1)
                if c == 0:
                    pe.wait_ge(consts_made, 1)
                if 0 < c < 7:
                    pe.wait_ge(node_kept, 8 + c)
                pe.wait_ge(attended_made, G - 1 if c < 6 else G)
                pe.wait_ge(lowest_made, G)
                for i in range(4):
                    last = pe.transpose(turned_place(c)[:, i * P:(i + 1) * P],
                                        nodes[:, 4 * c + i, 0:F], ident[:, :])
                last.then_inc(turned_done, 1)

            def node1(c):
                pe.wait_ge(turned_kept, c + 1)
                d_all, got = node1_places(c)
                last = pe.matmul(d_all, w_rep[1], turned_sb(c),
                                 start=True, stop=True)
                if c < 6:
                    last = node1_cols(c)
                last.then_inc(node_done, 1)

            def node1_cols(c):
                got = node1_places(c)[1]
                for i in range(4):
                    last = pe.matmul(got[:, 2 * i:2 * i + 2], turned_sb(c)[:, i * P:(i + 1) * P],
                                     w_cols[:, :], start=True, stop=True)
                return last

            def sum_values(layer):
                if layer == 0:
                    pe.wait_ge(tiles_kept, 16)
                else:
                    pe.wait_ge(node_kept, 8 + 9)
                pe.wait_ge(ones_made, 7)
                for t in range(T):
                    last = pe.matmul(acc[0:VW, 0, 0:1], values[layer][:, t, :], ones[:, 0:1],
                                     start=(t == 0), stop=(t == T - 1))
                last.then_inc(sum_col_done, 1)

            def spread_values(layer):
                pe.wait_ge(sum_rep_made, layer + 1)
                pe.wait_ge(row_turner_made, 4)
                pe.matmul(acc[:, 1, 0:VW], sum_rep,
                          ident[0:VW, 0:VW] if layer == 0 else turner[:, :],
                          start=True, stop=True).then_inc(sum_done, 1)

            def spread(n):
                pe.wait_ge(diag_made, n + 1)
                if n % G >= 2:
                    pe.wait_ge(attended_made, n - 1)
                if n == G:
                    pe.wait_ge(node_kept, 8 + 9)
                for b in range(2):
                    last = pe.matmul(misc[:, b, :], ones[:, :],
                                     s_row[:, n % 2, b * BANK:(b + 1) * BANK],
                                     start=True, stop=True)
                last.then_inc(spread_done, 1)

            def rows(n):
                pe.wait_ge(parts_made, n + 1)
                pe.wait_ge(spread_kept, n + 1)
                for k in range(GT):
                    last = pe.matmul(misc[0:3, k // 4, (k % 4) * P:(k % 4 + 1) * P],
                                     u_parts[:, k, :], ident_b[:, :], start=True, stop=True)
                last.then_inc(rows_done, 1)

            def fill_masks_first(n, slot):
                for k in range(GT):
                    pe.wait_ge(chunk_masked, 3 * (n * GT + k) + 1)
                    pe.matmul(work[slot][:, k * P:(k + 1) * P],
                              absent[:, (n % 2) * GT + k, slot * P:(slot + 1) * P],
                              minus_big[:, :], start=(k % 4 == 0), stop=False,
                              skip_group_check=True)

            def fill_rows_last(n, slot):
                mine = slice(64 * (n % 2), 64 * (n % 2) + 64)
                for b in range(2):
                    cols = slice(b * BANK, (b + 1) * BANK)
                    last = pe.matmul(work[slot][:, cols], pick[mine, :], u_rows[mine, cols],
                                     start=False, stop=True, skip_group_check=True)
                last.then_inc(filled, 1)

            def fill(n, jt, slot):
                pe.wait_ge(exped, n * T + jt - 1)
                mine = slice(64 * (n % 2), 64 * (n % 2) + 64)
                for b in range(2):
                    cols = slice(b * BANK, (b + 1) * BANK)
                    pe.matmul(work[slot][:, cols], pick[mine, :], u_rows[mine, cols],
                              start=True, stop=False)
                    for k in range(4 * b, 4 * b + 4):
                        last = pe.matmul(work[slot][:, k * P:(k + 1) * P],
                                         absent[:, (n % 2) * GT + k, bass.ds(jt * P, P)],
                                         minus_big[:, :], start=False, stop=(k % 4 == 3))
                last.then_inc(filled, 1)

            def use(n, jt, slot, first):
                pe.wait_ge(exped, n * T + jt + 1)
                for b in range(2):
                    if first and n > 0:
                        pe.wait_ge(acc_kept, 2 * n - 1 + b)
                    last = pe.matmul(acc[0:VW, b, :], values_now[:, slot, :],
                                     probs[:, slot, b * BANK:(b + 1) * BANK],
                                     start=first, stop=False, skip_group_check=True)
                last.then_inc(used, 1)

            def turn_acc(n):
                pe.wait_ge(acc_kept, 2 * (n + 1))
                for k in range(GT):
                    to = misc[:, k // 4, (k % 4) * VW:(k % 4 + 1) * VW]
                    mine = acc_sb[:, k * P:(k + 1) * P]
                    if n < G:
                        last = pe.transpose(to, mine, ident[0:VW, 0:VW])
                    else:
                        last = pe.matmul(to, mine, turner[:, :], start=True, stop=True)
                last.then_inc(acc_turned, 1)

            def steps(n, a, b):
                with pe.Fori(a // 2, b // 2) as q:
                    for i in range(2):
                        fill(n, q * 2 + i, i)
                        use(n, q * 2 + i - 2, i, False)

            entity_rows()
            tiles()
            for layer in range(2):
                if layer == 0:
                    sum_values(layer)
                    spread_values(layer)
                    spread(0)
                else:
                    sum_values(layer)
                    spread(G)
                    spread_values(layer)
                for g in range(G):
                    n = layer * G + g
                    if g == 0:
                        fill_masks_first(n, 0)
                        fill_masks_first(n, 1)
                        rows(n)
                        pe.wait_ge(rows_kept, n + 1)
                        fill_rows_last(n, 0)
                        fill_rows_last(n, 1)
                        pe.wait_ge(sum_kept, layer + 1)
                    else:
                        pe.wait_ge(rows_kept, n + 1)
                        for jt in range(2):
                            fill(n, jt, jt)
                            use(n - 1, T - 2 + jt, jt, False)
                    for jt in range(2, 4):
                        fill(n, jt, jt % 2)
                        use(n, jt - 2, jt % 2, jt == 2)
                    tasks = {4: (turn_acc, n - 1)} if g > 0 else {}
                    if g + 1 < G:
                        tasks[12], tasks[T - 2] = (spread, n + 1), (rows, n + 1)
                    if n == G - 1:
                        for c, at in enumerate(TURN_AT):
                            tasks[at], tasks[at + 2] = (turn_nodes, c), (node1, c)
                    done = 4
                    for at in sorted({*tasks, T}):
                        if at > done:
                            steps(n, done, at)
                        if at in tasks:
                            task, what = tasks[at]
                            task(what)
                        done = at
                for jt in range(T - 2, T):
                    use(layer * G + G - 1, jt, jt % 2, False)
                turn_acc(layer * G + G - 1)
                if layer == 0:
                    for c in (6, 7):
                        turn_nodes(c)
                    for c in (6, 7):
                        node1(c)
                    node1_cols(6)
                    node1_cols(7).then_inc(node_done, 1)


def kernel(x, adj, L0_gnn_entity_embs, L0_gnn_W, L0_gnn_a, L1_gnn_W, L1_gnn_a):
    import numpy as _np
    import concourse.bacc as _bacc
    from concourse import mybir as _mybir
    from concourse.bass_utils import run_bass_kernel_spmd as _run

    nc = _bacc.Bacc("TRN2", target_bir_lowering=False, num_devices=1)
    x, e = _np.asarray(x), _np.asarray(L0_gnn_entity_embs)
    w0, w1 = _np.asarray(L0_gnn_W), _np.asarray(L1_gnn_W)
    given = {
        "adj": _np.asarray(adj),
        "eT": e.T, "xT": x.T,
        "w0T": w0.T, "a0": _np.asarray(L0_gnn_a).reshape(2, -1).T,
        "w1": w1, "w1T": w1.T, "a1": _np.asarray(L1_gnn_a).reshape(2, -1).T,
    }
    arrays, args = {}, []
    for name, a in given.items():
        a = _np.ascontiguousarray(a)
        arrays[f"in_{name}_dram"] = a
        args.append(nc.dram_tensor(f"in_{name}_dram", a.shape, _mybir.dt.from_np(a.dtype),
                                   kind="ExternalInput").ap())
    out = nc.dram_tensor("out_dram", x.shape, _mybir.dt.from_np(x.dtype), kind="ExternalOutput").ap()
    two_attention_layers(nc, *args, out)
    return _run(nc, [arrays], core_ids=[0]).results[0]["out_dram"]
```

```python
from contextlib import ExitStack

import concourse.bass as bass
from concourse import mybir

ALU = mybir.AluOpType
ACT = mybir.ActivationFunctionType
AX = mybir.AxisListType
F32 = mybir.dt.float32
BF16 = mybir.dt.bfloat16
I32 = mybir.dt.int32
U8 = mybir.dt.uint8

P = 128
SLOPE = 0.2
EPS = 1e-5
SHRINK = 2.0 ** -40
BIG = 2.0 ** 60


def two_attention_layers(nc, adj, eT, xT, w0T, a0, w1, w1T, a1, out):
    F, N = xT.shape
    T = N // P
    GT = 8
    G = T // GT
    GW = GT * P
    C = -(-N // 3)
    CHUNKS = [(c, min(c + C, N)) for c in range(0, N, C)]
    BANK = 512
    FOURS = N // BANK
    NODE0 = FOURS
    NODE1 = NODE0 + FOURS + 1
    VW = F + 1
    SIX = 6
    LEAD = 3 * GT
    SEARCH = 27
    PIECE = -(-N * GT // SEARCH)
    SPREAD_AT = (7, 11)
    LAST_FOURS = (FOURS - 2, FOURS - 1)
    TURN_AT = (6, 10, 14, 18, 22, 26)

    with ExitStack() as ctx:
        def sb(name, shape, dt):
            return ctx.enter_context(nc.sbuf_tensor(name, shape, dt))

        def sem(name):
            return ctx.enter_context(nc.semaphore(name))

        absent = sb("absent", [P, 2 * GT, N], BF16)
        edges = sb("edges", [P, 3, C], I32)
        d_row = sb("d_row", [P, N], F32)
        s_row = sb("s_row", [P, 2, GW], F32)
        probs = sb("probs", [P, 2, GW], F32)
        nodes = sb("nodes", [P, T, VW], F32)
        entities = sb("entities", [P, T, VW], F32)
        values = [entities, nodes]
        results = [nodes, entities]
        values_now = sb("values_now", [P, 2, VW], F32)
        unused = sb("unused", [P, C], U8)
        u_row = sb("u_row", [P, GW], F32)
        attended = sb("attended", [P, GT, VW], F32)
        tmp = sb("tmp", [P, 2, GT, F], F32)
        tmp_a, tmp_b = tmp[:, 0, :, :], tmp[:, 1, :, :]
        tmp_flat = tmp[:, :, :, :].rearrange("p a k f -> p (a k f)")
        acc_sb = tmp_flat[0:VW, :]
        ident = sb("ident", [P, P], F32)
        minus_big = sb("minus_big", [P, P], BF16)
        ones = sb("ones", [P, P], F32)
        value_sum = sb("value_sum", [P, F], F32)
        d_col = sb("d_col", [P, 2, T], F32)
        nd8_col = sb("nd8_col", [P, 2, T], F32)
        s_col = sb("s_col", [P, T], F32)
        s8_col = sb("s8_col", [P, T], F32)
        low = sb("low", [P, GT, 5], F32)
        lowest = sb("lowest", [P, GT], F32)
        empty = sb("empty", [P, 2, GT], F32)
        guards = sb("guards", [P, 3, GT], F32)
        dens = sb("dens", [P, 2, GT], F32)
        stats = sb("stats", [P, 4, GT], F32)
        half_neg = sb("half_neg", [P, GT], F32)
        w0T_sb, w1_sb, w1T_sb = tmp_b[0:F, 0, :], tmp_b[0:F, 1, :], tmp_b[0:F, 3, :]
        a_sb = tmp_b[0:F, 2, 0:4].rearrange("f (l c) -> f l c", l=2)
        a_rep = tmp_a[0:F, 0:4, :].rearrange("f (l h) c -> f l (h c)", l=2)
        value_sum_T = attended[:, :, :].rearrange("p k f -> p (k f)")[0:F, 4 * VW:4 * VW + P]
        w_wide = attended[0:F, 0:2, :]
        w_rep = [tmp_b[0:F, 4:6, :].rearrange("f a b -> f (a b)"),
                 sb("w_rep", [F, P], F32)[:, :]]
        w_cols = sb("w_cols", [F, 2], F32)
        turner = sb("turner", [VW, VW], F32)

        work = [ctx.enter_context(nc.psum_tensor(f"work{i}", [P, GW], F32)) for i in range(2)]
        acc = ctx.enter_context(nc.psum_tensor("acc", [P, 2, BANK], F32))
        misc = ctx.enter_context(nc.psum_tensor("misc", [P, 2, BANK], F32))
        eT_sb = absent[0:F, GT:GT + 2, :].rearrange("p a b -> p (a b)").bitcast(F32)
        xT_sb = absent[0:F, GT + 2:GT + 4, :].rearrange("p a b -> p (a b)").bitcast(F32)
        spare = probs[:, 0, :].bitcast(U8).rearrange("p (s c) -> p s c", s=2)

        weights_in = sem("weights_in")
        eT_in = sem("eT_in")
        xT_in = sem("xT_in")
        chunk_in = [sem(f"chunk_in{i}") for i in range(3)]
        chunk_masked = sem("chunk_masked")
        consts_made = sem("consts_made")
        ones_made = sem("ones_made")
        reps_made = sem("reps_made")
        weights_done = sem("weights_done")
        weights_kept = sem("weights_kept")
        turner_made = sem("turner_made")
        turned_done = sem("turned_done")
        turned_kept = sem("turned_kept")
        node_done = sem("node_done")
        node_kept = sem("node_kept")
        values_added = sem("values_added")
        sum_T_done = sem("sum_T_done")
        sum_T_kept = sem("sum_T_kept")
        sum_done = sem("sum_done")
        sum_kept = sem("sum_kept")
        cols_made = sem("cols_made")
        row_low = sem("row_low")
        lowest_made = sem("lowest_made")
        pool_step = sem("pool_step")
        u_made = sem("u_made")
        u_diag_made = sem("u_diag_made")
        u_done = sem("u_done")
        u_kept = sem("u_kept")
        diag_made = sem("diag_made")
        spread_done = sem("spread_done")
        spread_kept = sem("spread_kept")
        filled = sem("filled")
        scored = sem("scored")
        exped = sem("exped")
        used = sem("used")
        acc_kept = sem("acc_kept")
        acc_turned = sem("acc_turned")
        attended_made = sem("attended_made")
        den_made = sem("den_made")
        neg_made = sem("neg_made")
        neg_exped = sem("neg_exped")
        y_made = sem("y_made")
        tiles_done = sem("tiles_done")
        tiles_kept = sem("tiles_kept")
        empty_made = sem("empty_made")
        guard_step = sem("guard_step")
        mean_made = sem("mean_made")
        square_made = sem("square_made")
        finish_step = sem("finish_step")
        spread_var_made = sem("spread_var_made")
        last_scale_made = sem("last_scale_made")
        var_made = sem("var_made")
        normed = sem("normed")
        stored = sem("stored")

        block = ctx.enter_context(nc.Block())

        def tiles_place(i):
            return (acc, misc)[i // 2 % 2][:, i % 2, 0:4 * VW].rearrange("p (t f) -> p t f", t=4)

        def turned_place(c):
            return misc[0:F, 0 if c < FOURS - 2 else c - LAST_FOURS[0], :]

        def turned_sb(c):
            if c < FOURS - 2:
                return d_row[0:F, c * BANK:(c + 1) * BANK]
            i = c - LAST_FOURS[0]
            return s_row[0:F, 1, i * BANK:(i + 1) * BANK]

        def node1_places(c):
            if c < FOURS - 2:
                return misc[:, 1, :], misc[:, 0, 0:8]
            i = c - LAST_FOURS[0]
            return work[0][:, i * BANK:(i + 1) * BANK], acc[:, i, 0:8]

        def by_tile(a):
            return a.rearrange("(t p) f -> p t f", p=P)

        @block.sync
        def _(sp):
            for to, frm in ((w0T_sb, w0T), (a_sb[:, 0, :], a0), (w1_sb, w1), (a_sb[:, 1, :], a1),
                            (w1T_sb, w1T)):
                sp.dma_start(to, frm).then_inc(weights_in, 16)
            sp.dma_start(eT_sb, eT).then_inc(eT_in, 16)

            def load_tile(layer, t, first):
                for c, (a, b) in enumerate(CHUNKS):
                    if not first:
                        sp.wait_ge(chunk_masked, 3 * T * layer + 3 * t + c - 2)
                    sp.dma_start(edges[:, c, 0:b - a], adj[bass.ds(t * P, P), a:b]
                                 ).then_inc(chunk_in[c], 16)

            load_tile(0, 0, True)
            sp.dma_start(xT_sb, xT).then_inc(xT_in, 16)
            with sp.Fori(1, T) as t:
                load_tile(0, t, False)
            with sp.Fori(0, T) as t:
                load_tile(1, t, False)
            for g in range(G):
                sp.wait_ge(normed, G + g + 1)
                sp.dma_start(by_tile(out)[:, g * GT:(g + 1) * GT, :],
                             results[1][:, g * GT:(g + 1) * GT, 0:F]).then_inc(stored, 16)
            sp.wait_ge(stored, 16 * G)

        @block.gpsimd
        def _(pool):
            steps = [0]

            def mine(ins):
                steps[0] += 1
                ins.then_inc(pool_step, 1)
                pool.wait_ge(pool_step, steps[0])

            mine(pool.memset(ident[:, :], 0.0))
            mine(pool.affine_select(out=ident[:, :], in_=ident[:, :], compare_op=ALU.not_equal,
                                    fill=1.0, base=0, pattern=[[-1, P]], channel_multiplier=1))
            mine(pool.tensor_scalar(minus_big[:, :], ident[:, :], -BIG, None, ALU.mult))
            pool.memset(half_neg[:, :], -0.5).then_inc(consts_made, 1)

            def columns(layer):
                if layer == 0:
                    pool.wait_ge(tiles_kept, 2 * FOURS)
                else:
                    pool.wait_ge(node_kept, NODE1)
                mine(pool.tensor_scalar(s8_col[:, :], s_col[:, :], 1 - SLOPE, None,
                                        ALU.mult))
                pool.tensor_scalar(nd8_col[:, layer, :], d_col[:, layer, :], -(1 - SLOPE), None,
                                   ALU.mult).then_inc(cols_made, 1)

            def add_values(layer):
                if layer == 0:
                    pool.wait_ge(tiles_kept, FOURS)
                else:
                    pool.wait_ge(normed, G)
                to = tmp_flat.rearrange("p (t f) -> p t f", f=F)
                rows, count = values[layer][:, :, 0:F], T // 2
                while count > 1:
                    mine(pool.tensor_tensor(to[:, 0:count, :], rows[:, 0:count, :],
                                            rows[:, count:2 * count, :], ALU.add))
                    rows, count = to, count // 2
                pool.tensor_tensor(to[:, 0, :], to[:, 0, :], to[:, 1, :],
                                   ALU.add).then_inc(values_added, 1)

            def diagonal(layer, g):
                n = layer * G + g
                if n >= 2:
                    pool.wait_ge(scored, T * (n - 1))
                pool.tensor_tensor(
                    s_row[:, n % 2, :].rearrange("p (k q) -> p k q", k=GT),
                    ident[:, :].unsqueeze(1).to_broadcast([P, GT, P]),
                    s8_col[:, g * GT:(g + 1) * GT].unsqueeze(2).to_broadcast([P, GT, P]),
                    ALU.mult).then_inc(diag_made, 1)

            def u_diagonal(n):
                pool.wait_ge(u_made, n + 1)
                pool.tensor_tensor(
                    tmp_flat.rearrange("p (k q) -> p k q", k=GT),
                    ident[:, :].unsqueeze(1).to_broadcast([P, GT, P]),
                    guards[:, 2, :].unsqueeze(2).to_broadcast([P, GT, P]),
                    ALU.mult).then_inc(u_diag_made, 1)

            def wide(column):
                return column.unsqueeze(2).to_broadcast([P, GT, F])

            def row_sums(rows, stat):
                width = F // 2
                while width > 1:
                    mine(pool.tensor_tensor(tmp_a[:, :, 0:width], rows[:, :, 0:width],
                                            rows[:, :, width:2 * width], ALU.add))
                    rows, width = tmp_a, width // 2
                mine(pool.tensor_tensor(stats[:, stat, :], rows[:, :, 0], rows[:, :, 1], ALU.add))

            def finish(layer, g):
                n = layer * G + g
                here = nodes[:, g * GT:(g + 1) * GT, 0:F]
                to = results[layer][:, g * GT:(g + 1) * GT, 0:F]
                pool.wait_ge(attended_made, n + 1)
                pool.wait_ge(sum_kept, layer + 1)
                pool.wait_ge(empty_made, n + 1)
                mine(pool.tensor_tensor(
                    tmp_a[:, :, :], value_sum[:, 0:F].unsqueeze(1).to_broadcast([P, GT, F]),
                    wide(empty[:, n % 2, :]), ALU.mult))
                mine(pool.tensor_tensor(tmp_b[:, :, :], attended[:, :, 0:F], tmp_a[:, :, :], ALU.add))
                pool.wait_ge(den_made, 2 * (n + 1))
                mine(pool.tensor_tensor(tmp_a[:, :, :], tmp_b[:, :, :], wide(dens[:, 1, :]), ALU.mult))
                h, other = tmp_a, tmp_b
                if layer == 0:
                    mine(pool.tensor_tensor(tmp_b[:, :, :], tmp_a[:, :, :], here, ALU.add))
                    h, other = tmp_b, tmp_a
                pool.tensor_scalar(other[:, :, :], h[:, :, :], 0.0, None, ALU.min).then_inc(neg_made, 1)
                mine(pool.tensor_scalar(h[:, :, :], h[:, :, :], 0.0, -1.0, ALU.max, ALU.add))
                pool.wait_ge(neg_exped, n + 1)
                mine(pool.tensor_tensor(h[:, :, :], h[:, :, :], other[:, :, :], ALU.add))
                mine(pool.tensor_tensor(to, here, h[:, :, :], ALU.add))
                row_sums(to, 0)
                mine(pool.tensor_scalar(stats[:, 1, :], stats[:, 0, :], 1.0 / F, None, ALU.mult))
                mine(pool.tensor_tensor(to, to, wide(stats[:, 1, :]), ALU.subtract))
                mine(pool.tensor_tensor(tmp_b[:, :, :], to, to, ALU.mult))
                row_sums(tmp_b, 2)
                mine(pool.tensor_scalar(stats[:, 3, :], stats[:, 2, :], 1.0 / F, EPS, ALU.mult,
                                        ALU.add))
                mine(pool.tensor_tensor(stats[:, 1, :], stats[:, 3, :], half_neg[:, :], ALU.pow))
                pool.tensor_tensor(to, to, wide(stats[:, 1, :]), ALU.mult).then_inc(normed, 1)
                pool.wait_ge(normed, n + 1)

            for layer in range(2):
                add_values(layer)
                columns(layer)
                diagonal(layer, 0)
                for g in range(G):
                    if g + 1 < G:
                        diagonal(layer, g + 1)
                    if g > 0:
                        finish(layer, g - 1)
                    if g + 1 < G:
                        u_diagonal(layer * G + g + 1)
                pool.wait_ge(spread_var_made, layer + 1)
                pool.tensor_tensor(stats[:, 1, :], stats[:, 3, :], half_neg[:, :],
                                   ALU.pow).then_inc(last_scale_made, 1)

        @block.scalar
        def _(act):
            def mask_chunk(layer, t, k, c):
                a, b = CHUNKS[c]
                act.wait_ge(chunk_in[c], 16 * T * layer + 16 * (t + 1))
                nc.scalar.activation(absent[:, k, a:b], edges[:, c, 0:b - a],
                                     ACT.Relu, bias=1.0, scale=-1.0).then_inc(chunk_masked, 1)

            def exp_step(layer, g, jt, slot, wait_used):
                n = layer * G + g
                act.wait_ge(filled, n * T + jt + 1)
                if wait_used:
                    act.wait_ge(used, n * T + jt - 1)
                nc.scalar.copy(values_now[:, slot, :], values[layer][:, bass.ds(jt, 1), :]
                               .rearrange("p a f -> p (a f)"))
                nc.scalar.activation(probs[:, slot, :], work[slot][:, :], ACT.Exp,
                                     bias=d_col[:, layer, bass.ds(jt, 1)]).then_inc(exped, 1)

            def keep_node1(c):
                tiles = slice(4 * c, 4 * c + 4)
                act.wait_ge(node_done, NODE0 + c + 1)
                d_all, got = node1_places(c)
                got = got.rearrange("p (t c) -> p t c", t=4)
                ins = nc.scalar.mul(d_row[:, c * BANK:(c + 1) * BANK], d_all, -SHRINK)
                if c >= FOURS - 2:
                    ins.then_inc(node_kept, 1)
                    return
                nc.scalar.copy(d_col[:, 1, tiles], got[:, :, 0])
                nc.scalar.copy(s_col[:, tiles], got[:, :, 1]).then_inc(node_kept, 1)

            def keep_last_cols():
                act.wait_ge(node_done, NODE1)
                for c in LAST_FOURS:
                    tiles = slice(4 * c, 4 * c + 4)
                    got = node1_places(c)[1].rearrange("p (t c) -> p t c", t=4)
                    nc.scalar.copy(d_col[:, 1, tiles], got[:, :, 0])
                    last = nc.scalar.copy(s_col[:, tiles], got[:, :, 1])
                last.then_inc(node_kept, 1)

            def keep_spread(n, b):
                act.wait_ge(spread_done, 2 * n + b + 1)
                nc.scalar.copy(s_row[:, n % 2, b * BANK:(b + 1) * BANK], misc[:, b, :]
                               ).then_inc(spread_kept, 1)

            def keep_sum(layer):
                act.wait_ge(sum_T_done, layer + 1)
                nc.scalar.copy(value_sum_T, misc[0:F, 0, 0:P]).then_inc(sum_T_kept, 1)
                act.wait_ge(sum_done, layer + 1)
                nc.scalar.copy(value_sum[:, :], misc[:, 1, 0:F]).then_inc(sum_kept, 1)

            def keep_acc(n):
                act.wait_ge(used, T * (n + 1))
                if n > 0:
                    act.wait_ge(normed, n)
                nc.scalar.copy(acc_sb[:, BANK:GW], acc[0:VW, 1, :]).then_inc(acc_kept, 1)

            def keep_attended(n):
                act.wait_ge(acc_turned, n + 1)
                nc.scalar.copy(attended[:, :, :].rearrange("p (a k) f -> p a (k f)", a=2),
                               misc[:, :, 0:4 * VW]).then_inc(attended_made, 1)

            def exp_neg(layer, g):
                n = layer * G + g
                act.wait_ge(neg_made, n + 1)
                it = tmp_a if layer == 0 else tmp_b
                nc.scalar.activation(it[:, :, :], it[:, :, :], ACT.Exp).then_inc(neg_exped, 1)

            def group(layer, g):
                n = layer * G + g
                nxt = n + 1
                incoming = nxt < 2 * G
                nlayer, ng = nxt // G, nxt % G
                if incoming and nxt >= 2:
                    act.wait_ge(filled, T * (nxt - 1))

                def six(q, after, late={}, start=False):
                    for i in range(SIX):
                        exp_step(layer, g, q * SIX + i, i % 2, n > 0 or not start or i > 1)
                        for task in after.get(i, ()):
                            task()
                        if incoming:
                            k = q * 2 + i // 3
                            mask_chunk(nlayer, k + ng * GT, k + (nxt % 2) * GT, i % 3)
                        for task in late.get(i, ()):
                            task()

                early = {}
                if g > 0:
                    early[0] = (lambda: keep_acc(n - 1),)
                    early[4] = (lambda: keep_attended(n - 1),)
                six(0, early, start=True)
                if n == G - 1:
                    after = {at + 2: c for c, at in enumerate(TURN_AT)}
                    for q in range(1, LEAD // SIX):
                        six(q, {3: (lambda: exp_neg(layer, g - 1),)} if q == 1 else {},
                            {i: (lambda c=after[q * SIX + i]: keep_node1(c),)
                             for i in range(SIX) if q * SIX + i in after})
                    for jt in range(LEAD, T):
                        exp_step(layer, g, jt, jt % 2, True)
                        if jt in after:
                            keep_node1(after[jt])
                    return
                later = {}
                if g + 1 < G:
                    for b, at in enumerate(SPREAD_AT):
                        later[at - SIX] = (lambda b=b: keep_spread(n + 1, b),)
                if g > 0:
                    later[3] = (lambda: exp_neg(layer, g - 1),)
                six(1, later)
                with act.Fori(2, GT // 2) as q:
                    six(q, {})
                with act.Fori(LEAD // 2, T // 2) as q:
                    for i in range(2):
                        exp_step(layer, g, q * 2 + i, i, True)

            def keep_tiles(i):
                tiles = slice(i % FOURS * 4, i % FOURS * 4 + 4)
                to, col = ((entities, d_col[:, 0, :]), (nodes, s_col))[i // FOURS]
                act.wait_ge(tiles_done, i + 1)
                nc.scalar.copy(to[:, tiles, 0:F], tiles_place(i)[:, :, 0:F])
                nc.scalar.copy(col[:, tiles], tiles_place(i)[:, :, F]).then_inc(tiles_kept, 1)

            def mask_tile(k):
                for c in range(3):
                    mask_chunk(0, k, k, c)

            mask_tile(0)
            mask_tile(1)
            for k in range(2, 6):
                mask_tile(k)
                for i in range(4 * k - 8, 4 * k - 4):
                    keep_tiles(i)
            with act.Fori(6, GT) as k:
                mask_tile(k)
            act.wait_ge(ones_made, 3)
            for layer in range(2):
                keep_sum(layer)
                for b in range(2):
                    keep_spread(layer * G, b)
                for g in range(G):
                    group(layer, g)
                keep_acc(layer * G + G - 1)
                keep_attended(layer * G + G - 1)
                exp_neg(layer, G - 1)
                if layer == 0:
                    for c in LAST_FOURS:
                        keep_node1(c)
                    keep_last_cols()

        @block.vector
        def _(dve):
            dve.memset(ones[:, :], 1.0).then_inc(ones_made, 1)
            dve.memset(low[:, :, :], BIG).then_inc(row_low, 1)
            dve.wait_ge(ones_made, 1)
            dve.wait_ge(weights_in, 16 * 5)
            for layer in range(2):
                dve.tensor_scalar(a_rep[:, layer, :], ones[0:F, :], a_sb[:, layer, 1:2], None,
                                  ALU.mult).then_inc(reps_made, 1)
            dve.wait_ge(consts_made, 1)
            for i in range(2):
                dve.tensor_copy(w_wide[:, i, 0:F], ident[0:F, 0:F])
            dve.wait_ge(weights_done, 1)
            for layer in range(2):
                dve.tensor_copy(w_rep[layer], misc[0:F, 0, layer * P:(layer + 1) * P])
            dve.tensor_copy(w_cols[:, 0:1], misc[0:F, 0, P:P + 1])
            dve.tensor_copy(w_cols[:, 1:2], misc[0:F, 0, 2 * P + 1:2 * P + 2])
            dve.tensor_copy(w_wide[:, 0, F:VW], misc[0:F, 0, 0:1])
            dve.tensor_copy(w_wide[:, 1, F:VW],
                            misc[0:F, 0, 2 * P:2 * P + 1]).then_inc(weights_kept, 1)
            dve.tensor_copy(turner[0:F, 0:F], w1T_sb).then_inc(turner_made, 1)
            dve.memset(turner[0:F, F:VW], 0.0).then_inc(turner_made, 1)
            dve.memset(turner[F:VW, 0:F], 0.0).then_inc(turner_made, 1)
            dve.memset(turner[F:VW, F:VW], 1.0).then_inc(turner_made, 1)
            dve.memset(entities[:, :, F:VW], 1.0).then_inc(ones_made, 1)
            dve.memset(nodes[:, :, F:VW], 1.0).then_inc(ones_made, 1)

            pieces = [1]

            def lowest_of_piece(n, k, piece, start, end, probs_free=False, beside=0):
                dve.wait_ge(chunk_masked, 3 * (n * GT + k) + -(-end // C))
                if not beside:
                    dve.wait_ge(row_low, max(1, pieces[0] - probs_free))
                out = spare[:, pieces[0] % 2, :] if probs_free else unused[:, beside:C]
                dve.tensor_tensor_reduce(
                    out=out[:, 0:end - start], in0=absent[:, (n % 2) * GT + k, start:end],
                    in1=d_row[:, start:end], scale=1.0, scalar=BIG, op0=ALU.add, op1=ALU.min,
                    accum_out=low[:, k, piece:piece + 1]).then_inc(row_low, 1)
                pieces[0] += 1

            def search(n, jt):
                step = jt - 2
                first, end = step * PIECE, min((step + 1) * PIECE, GT * N)
                at = first
                while at < end:
                    k, start = divmod(at, N)
                    stop = min(N, start + end - at)
                    lowest_of_piece(n, k, step - k * N // PIECE, start, stop, beside=at - first)
                    at += stop - start

            def lowest_of_group(n):
                dve.wait_ge(row_low, pieces[0])
                dve.tensor_reduce(lowest[:, :], low[:, :, :], AX.X, ALU.min).then_inc(lowest_made, 1)
                dve.wait_ge(lowest_made, n + 1)
                dve.memset(low[:, :, :], BIG).then_inc(row_low, 1)
                pieces[0] += 1

            guard_steps = [0]

            def guard(layer, g):
                n = layer * G + g
                s = s_col[:, g * GT:(g + 1) * GT]
                highest, m, u = (guards[:, i, :] for i in range(3))

                def mine(ins):
                    guard_steps[0] += 1
                    ins.then_inc(guard_step, 1)
                    dve.wait_ge(guard_step, guard_steps[0])

                dve.wait_ge(lowest_made, n + 1)
                if n >= 1:
                    dve.wait_ge(u_diag_made, n)
                dve.tensor_scalar(empty[:, n % 2, :], lowest[:, :], 0.5, None,
                                  ALU.is_gt).then_inc(empty_made, 1)
                mine(dve.scalar_tensor_tensor(out=highest, in0=lowest[:, :], scalar=-1.0 / SHRINK,
                                              in1=s, op0=ALU.mult, op1=ALU.add))
                mine(dve.scalar_tensor_tensor(out=m, in0=highest, scalar=SLOPE, in1=highest,
                                              op0=ALU.mult, op1=ALU.max))
                dve.scalar_tensor_tensor(out=u, in0=s, scalar=SLOPE, in1=m,
                                         op0=ALU.mult, op1=ALU.subtract).then_inc(u_made, 1)

            def u_diagonal(n):
                dve.wait_ge(u_made, n + 1)
                dve.wait_ge(consts_made, 1)
                dve.wait_ge(sum_T_done, n // G + 1)
                dve.tensor_tensor(
                    tmp_flat.rearrange("p (k q) -> p k q", k=GT),
                    ident[:, :].unsqueeze(1).to_broadcast([P, GT, P]),
                    guards[:, 2, :].unsqueeze(2).to_broadcast([P, GT, P]),
                    ALU.mult).then_inc(u_diag_made, 1)

            def keep_u(n):
                if n >= 1:
                    dve.wait_ge(scored, T * n)
                for b in range(2):
                    dve.wait_ge(u_done, 2 * n + b + 1)
                    dve.tensor_copy(u_row[:, b * BANK:(b + 1) * BANK], misc[:, b, :]
                                    ).then_inc(u_kept, 1)
                dve.wait_ge(u_kept, 2 * (n + 1))

            def score_step(layer, g, jt):
                n = layer * G + g
                step = n * T + jt
                if step >= 2:
                    dve.wait_ge(exped, step - 1)
                dve.scalar_tensor_tensor(out=work[jt % 2][:, :], in0=s_row[:, n % 2, :],
                                         scalar=nd8_col[:, layer, jt:jt + 1], in1=u_row[:, :],
                                         op0=ALU.max, op1=ALU.add).then_inc(scored, 1)

            def denominator(layer, g):
                n = layer * G + g
                dve.wait_ge(attended_made, n + 1)
                dve.scalar_tensor_tensor(out=dens[:, 0, :], in0=empty[:, n % 2, :], scalar=float(N),
                                         in1=attended[:, :, F], op0=ALU.mult,
                                         op1=ALU.add).then_inc(den_made, 1)
                dve.wait_ge(den_made, 2 * n + 1)
                dve.reciprocal(dens[:, 1, :], dens[:, 0, :]).then_inc(den_made, 1)

            def row_sums(layer, g, second):
                n = layer * G + g
                if not second:
                    dve.wait_ge(y_made, layer + 1)
                    dve.tensor_reduce(stats[:, 0, :], results[layer][:, g * GT:(g + 1) * GT, 0:F], AX.X,
                                      ALU.add).then_inc(mean_made, 1)
                else:
                    dve.wait_ge(square_made, layer + 1)
                    dve.tensor_reduce(stats[:, 2, :], tmp_a[:, :, :], AX.X,
                                      ALU.add).then_inc(var_made, 1)

            def keep_acc(n):
                dve.wait_ge(used, T * (n + 1))
                if n > 0:
                    dve.wait_ge(normed, n)
                dve.tensor_copy(acc_sb[:, 0:BANK], acc[0:VW, 0, :]).then_inc(acc_kept, 1)

            def keep_turned(c):
                dve.wait_ge(turned_done, c + 1)
                dve.tensor_copy(turned_sb(c), turned_place(c)).then_inc(turned_kept, 1)

            finish_steps = [0]

            def mine(ins):
                finish_steps[0] += 1
                ins.then_inc(finish_step, 1)
                dve.wait_ge(finish_step, finish_steps[0])

            def wide(column, width=F):
                return column.unsqueeze(2).to_broadcast([P, GT, width])

            def finish_last(layer, between):
                n = layer * G + G - 1
                here = nodes[:, (G - 1) * GT:T, 0:F]
                to = results[layer][:, (G - 1) * GT:T, 0:F]
                all_alike = s_row[:, (n + 1) % 2, 0:GT * F].rearrange("p (k f) -> p k f", k=GT)
                mine(dve.tensor_tensor(
                    all_alike, value_sum[:, 0:F].unsqueeze(1).to_broadcast([P, GT, F]),
                    wide(empty[:, n % 2, :]), ALU.mult))
                between(0)
                keep_acc(n)
                between(1)
                denominator(layer, G - 1)
                mine(dve.tensor_tensor(tmp_b[:, :, :], attended[:, :, 0:F], all_alike, ALU.add))
                dve.wait_ge(den_made, 2 * (n + 1))
                mine(dve.tensor_tensor(tmp_a[:, :, :], tmp_b[:, :, :], wide(dens[:, 1, :]), ALU.mult))
                h, other = tmp_a, tmp_b
                if layer == 0:
                    mine(dve.tensor_tensor(tmp_b[:, :, :], tmp_a[:, :, :], here, ALU.add))
                    h, other = tmp_b, tmp_a
                dve.tensor_scalar(other[:, :, :], h[:, :, :], 0.0, None, ALU.min).then_inc(neg_made, 1)
                mine(dve.scalar_tensor_tensor(out=h[:, :, :], in0=h[:, :, :], scalar=0.0, in1=here,
                                              op0=ALU.max, op1=ALU.add))
                dve.wait_ge(neg_exped, n + 1)
                dve.scalar_tensor_tensor(out=to, in0=other[:, :, :], scalar=-1.0, in1=h[:, :, :],
                                         op0=ALU.add, op1=ALU.add).then_inc(y_made, 1)
                row_sums(layer, G - 1, False)
                dve.wait_ge(mean_made, layer + 1)
                mine(dve.tensor_scalar(stats[:, 1, :], stats[:, 0, :], 1.0 / F, None, ALU.mult))
                mine(dve.tensor_tensor(to, to, wide(stats[:, 1, :]), ALU.subtract))
                dve.tensor_tensor(tmp_a[:, :, :], to, to, ALU.mult).then_inc(square_made, 1)
                row_sums(layer, G - 1, True)
                dve.wait_ge(var_made, layer + 1)
                dve.tensor_scalar(stats[:, 3, :], stats[:, 2, :], 1.0 / F, EPS, ALU.mult,
                                  ALU.add).then_inc(spread_var_made, 1)
                between(2)
                dve.wait_ge(last_scale_made, layer + 1)
                dve.tensor_tensor(to, to, wide(stats[:, 1, :]), ALU.mult).then_inc(normed, 1)

            CUTS = [0, 2 * BANK, 4 * BANK, 6 * BANK, N]
            for layer in range(2):
                if layer == 0:
                    for c in range(FOURS):
                        dve.wait_ge(node_done, c + 1)
                        dve.tensor_scalar(d_row[:, c * BANK:(c + 1) * BANK],
                                          work[c // 2 % 2][:, c % 2 * BANK:(c % 2 + 1) * BANK],
                                          -SHRINK, None, ALU.mult).then_inc(node_kept, 1)
                    dve.wait_ge(node_kept, NODE0)
                    for k in range(GT):
                        for c, (a, b) in enumerate(CHUNKS):
                            lowest_of_piece(0, k, c, a, b, True)
                    lowest_of_group(0)
                    dve.wait_ge(tiles_kept, 2 * FOURS)
                    guard(0, 0)
                    u_diagonal(0)
                dve.wait_ge(cols_made, layer + 1)
                for g in range(G):
                    n = layer * G + g
                    dve.wait_ge(spread_kept, 2 * (n + 1))
                    keep_u(n)
                    for jt in range(T):
                        score_step(layer, g, jt)
                        if g > 0 and jt == 1:
                            keep_acc(n - 1)
                        if g > 0 and jt == 6:
                            denominator(layer, g - 1)
                        if g + 1 < G and 2 <= jt < 2 + SEARCH:
                            search(n + 1, jt)
                        if g + 1 < G and jt == 1 + SEARCH:
                            lowest_of_group(n + 1)
                            guard(layer, g + 1)
                        if n == G - 1:
                            if jt - 1 in TURN_AT:
                                keep_turned(TURN_AT.index(jt - 1))
                            if jt in (16, 24):
                                dve.wait_ge(node_kept, NODE0 + (jt - 8) // 4)
                            if jt >= 16:
                                piece, k = divmod(jt - 16, GT)
                                lowest_of_piece(G, k, piece, CUTS[piece], CUTS[piece + 1])

                def search_on(gap):
                    if layer == 0:
                        for k in ((0, 1, 2), (3,), (4,))[gap]:
                            dve.wait_ge(node_kept, NODE0 + FOURS - 2)
                            lowest_of_piece(G, k, 2, CUTS[2], CUTS[3])

                finish_last(layer, search_on)
                if layer == 0:
                    for c in LAST_FOURS:
                        keep_turned(c)
                    for k in range(5, GT):
                        lowest_of_piece(G, k, 2, CUTS[2], CUTS[3], True)
                    dve.wait_ge(node_kept, NODE0 + FOURS)
                    for k in range(GT):
                        lowest_of_piece(G, k, 3, CUTS[3], CUTS[4], True)
                    lowest_of_group(G)
                    guard(1, 0)
                    u_diagonal(G)

        @block.tensor
        def _(pe):
            pe.wait_ge(ones_made, 1)
            pe.wait_ge(weights_in, 16 * 5)
            pe.wait_ge(reps_made, 2)
            for layer, w in ((0, w0T_sb), (1, w1_sb)):
                pe.matmul(misc[0:F, 0, layer * P:(layer + 1) * P], w, a_rep[:, layer, :],
                          start=True, stop=True)
            for layer, w in ((0, w0T_sb), (1, w1_sb)):
                last = pe.matmul(misc[0:F, 0, 2 * P + layer:2 * P + layer + 1], w,
                                 a_sb[:, layer, 0:1], start=True, stop=True)
            last.then_inc(weights_done, 1)
            pe.wait_ge(weights_kept, 1)
            pe.wait_ge(eT_in, 16)

            def entity_rows():
                for c in range(FOURS):
                    if c >= 4:
                        pe.wait_ge(node_kept, c - 3)
                    pe.matmul(work[c // 2 % 2][:, c % 2 * BANK:(c % 2 + 1) * BANK], w_rep[0],
                              eT_sb[:, c * BANK:(c + 1) * BANK],
                              start=True, stop=True).then_inc(node_done, 1)

            def tiles():
                for i in range(2 * FOURS):
                    if i == FOURS:
                        pe.wait_ge(xT_in, 16)
                    if i >= 4:
                        pe.wait_ge(tiles_kept, i - 3)
                    for t in range(4):
                        at = (i % FOURS * 4 + t) * P
                        last = pe.matmul(tiles_place(i)[:, t, :],
                                         (eT_sb, xT_sb)[i // FOURS][:, at:at + P],
                                         w_wide[:, i // FOURS, :], start=True, stop=True)
                    last.then_inc(tiles_done, 1)

            def turn_nodes(c):
                pe.wait_ge(normed, c // 2 + 1)
                if c == 0:
                    pe.wait_ge(consts_made, 1)
                if 0 < c < FOURS - 1:
                    pe.wait_ge(node_kept, NODE0 + c)
                pe.wait_ge(attended_made, G - 1 if c < FOURS - 2 else G)
                pe.wait_ge(lowest_made, G)
                for i in range(4):
                    last = pe.transpose(turned_place(c)[:, i * P:(i + 1) * P],
                                        nodes[:, 4 * c + i, 0:F], ident[:, :])
                last.then_inc(turned_done, 1)

            def node1(c):
                pe.wait_ge(turned_kept, c + 1)
                d_all, got = node1_places(c)
                last = pe.matmul(d_all, w_rep[1], turned_sb(c),
                                 start=True, stop=True)
                if c < FOURS - 2:
                    last = node1_cols(c)
                last.then_inc(node_done, 1)

            def node1_cols(c):
                got = node1_places(c)[1]
                for i in range(4):
                    last = pe.matmul(got[:, 2 * i:2 * i + 2], turned_sb(c)[:, i * P:(i + 1) * P],
                                     w_cols[:, :], start=True, stop=True)
                return last

            def sum_values(layer):
                pe.wait_ge(values_added, layer + 1)
                if layer == 0:
                    pe.wait_ge(tiles_kept, 2 * FOURS)
                pe.matmul(misc[0:F, 0, 0:P], tmp_flat[:, 0:F], ones[:, :],
                          start=True, stop=True).then_inc(sum_T_done, 1)
                pe.wait_ge(sum_T_kept, layer + 1)
                pe.wait_ge(turner_made, 4)
                pe.matmul(misc[:, 1, 0:F], value_sum_T,
                          (ident if layer == 0 else turner)[0:F, 0:F],
                          start=True, stop=True).then_inc(sum_done, 1)

            def spread(n, b):
                pe.wait_ge(diag_made, n + 1)
                if n % G >= 2:
                    pe.wait_ge(attended_made, n - 1)
                if n % G == 0:
                    pe.wait_ge(sum_kept, n // G + 1)
                if n == G:
                    pe.wait_ge(node_kept, NODE1)
                pe.matmul(misc[:, b, :], ones[:, :], s_row[:, n % 2, b * BANK:(b + 1) * BANK],
                          start=True, stop=True).then_inc(spread_done, 1)

            def spread_u(n):
                pe.wait_ge(u_diag_made, n + 1)
                pe.wait_ge(spread_kept, 2 * (n + 1))
                for b in range(2):
                    pe.matmul(misc[:, b, :], ones[:, :], tmp_flat[:, b * BANK:(b + 1) * BANK],
                              start=True, stop=True).then_inc(u_done, 1)

            def fill(n, jt, slot):
                pe.wait_ge(scored, n * T + jt + 1)
                for k in range(GT):
                    last = pe.matmul(work[slot][:, k * P:(k + 1) * P],
                                     absent[:, (n % 2) * GT + k, bass.ds(jt * P, P)],
                                     minus_big[:, :], start=False, stop=True,
                                     skip_group_check=True)
                last.then_inc(filled, 1)

            def use(n, jt, slot, first):
                pe.wait_ge(exped, n * T + jt + 1)
                if first and n > 0:
                    pe.wait_ge(acc_kept, 2 * n)
                for b in range(2):
                    last = pe.matmul(acc[0:VW, b, :], values_now[:, slot, :],
                                     probs[:, slot, b * BANK:(b + 1) * BANK],
                                     start=first, stop=False, skip_group_check=True)
                last.then_inc(used, 1)

            def turn_acc(n):
                pe.wait_ge(acc_kept, 2 * (n + 1))
                if n % G < G - 1:
                    pe.wait_ge(u_kept, 2 * (n + 2))
                for k in range(GT):
                    to = misc[:, k // 4, (k % 4) * VW:(k % 4 + 1) * VW]
                    mine = acc_sb[:, k * P:(k + 1) * P]
                    if n < G:
                        last = pe.transpose(to, mine, ident[0:VW, 0:VW])
                    else:
                        last = pe.matmul(to, mine, turner[:, :], start=True, stop=True)
                last.then_inc(acc_turned, 1)

            def steps(n, a, b):
                if a % 2:
                    fill(n, a, 1)
                    use(n, a - 1, 0, False)
                    a += 1
                if b - a >= 2:
                    with pe.Fori(a // 2, b // 2) as q:
                        for i in range(2):
                            fill(n, q * 2 + i, i)
                            use(n, q * 2 + i - 1, 1 - i, False)
                if (b - a) % 2:
                    fill(n, b - 1, 0)
                    use(n, b - 2, 1, False)

            entity_rows()
            tiles()
            for layer in range(2):
                sum_values(layer)
                for b in range(2):
                    spread(layer * G, b)
                spread_u(layer * G)
                for g in range(G):
                    n = layer * G + g
                    fill(n, 0, 0)
                    if g > 0:
                        use(n - 1, T - 1, 1, False)
                    fill(n, 1, 1)
                    use(n, 0, 0, True)
                    tasks = {4: (turn_acc, n - 1)} if g > 0 else {}
                    if g + 1 < G:
                        for b, at in enumerate(SPREAD_AT):
                            tasks[at] = (spread, n + 1, b)
                        tasks[T - 2] = (spread_u, n + 1)
                    if n == G - 1:
                        for c, at in enumerate(TURN_AT):
                            tasks[at], tasks[at + 3] = (turn_nodes, c), (node1, c)
                    done = 2
                    for at in sorted({*tasks, T}):
                        if at > done:
                            steps(n, done, at)
                        if at in tasks:
                            task, *what = tasks[at]
                            task(*what)
                        done = at
                use(layer * G + G - 1, T - 1, 1, False)
                turn_acc(layer * G + G - 1)
                if layer == 0:
                    for c in LAST_FOURS:
                        turn_nodes(c)
                    for c in LAST_FOURS:
                        node1(c)
                    for c in LAST_FOURS:
                        last = node1_cols(c)
                    last.then_inc(node_done, 1)


def kernel(x, adj, L0_gnn_entity_embs, L0_gnn_W, L0_gnn_a, L1_gnn_W, L1_gnn_a):
    import numpy as _np
    import concourse.bacc as _bacc
    from concourse import mybir as _mybir
    from concourse.bass_utils import run_bass_kernel_spmd as _run

    nc = _bacc.Bacc("TRN2", target_bir_lowering=False, num_devices=1)
    x, e = _np.asarray(x), _np.asarray(L0_gnn_entity_embs)
    w0, w1 = _np.asarray(L0_gnn_W), _np.asarray(L1_gnn_W)
    given = {
        "adj": _np.asarray(adj),
        "eT": e.T, "xT": x.T,
        "w0T": w0.T, "a0": _np.asarray(L0_gnn_a).reshape(2, -1).T,
        "w1": w1, "w1T": w1.T, "a1": _np.asarray(L1_gnn_a).reshape(2, -1).T,
    }
    arrays, args = {}, []
    for name, a in given.items():
        a = _np.ascontiguousarray(a)
        arrays[f"in_{name}_dram"] = a
        args.append(nc.dram_tensor(f"in_{name}_dram", a.shape, _mybir.dt.from_np(a.dtype),
                                   kind="ExternalInput").ap())
    out = nc.dram_tensor("out_dram", x.shape, _mybir.dt.from_np(x.dtype), kind="ExternalOutput").ap()
    two_attention_layers(nc, *args, out)
    return _run(nc, [arrays], core_ids=[0]).results[0]["out_dram"]
```
